# Optimizing a Trainium2 kernel written in Bass

```python
import numpy as np
import jax
import jax.numpy as jnp

def _softmax(x, axis=-1):
    return jax.nn.softmax(x, axis=axis)

def _gelu(x):
    return jax.nn.gelu(x, approximate=True)

def _silu(x):
    return jax.nn.silu(x)

def _sigmoid(x):
    return jax.nn.sigmoid(x)

def _layernorm(x, axis=-1, eps=1e-05):
    m = jnp.mean(x, axis=axis, keepdims=True)
    v = jnp.var(x, axis=axis, keepdims=True)
    return (x - m) / jnp.sqrt(v + eps)

def _scatter_add(tgt, idx, src, axis=0):
    return tgt.at[idx].add(src)

def _segment_sum(src, seg, n):
    return jax.ops.segment_sum(src, seg, n)
kernel_name = 'mk_gnn_ffn_d1_gnn_r8_fc1e0b'

def setup_inputs(seed: int=0):
    np.random.seed(seed)
    _w = jnp.asarray

    def _rec_inputs():
        import jax
        import jax.numpy as jnp
        _gk = jax.random.key(seed)
        x = -0.0003713 + 1 * jax.random.normal(jax.random.fold_in(_gk, 1), (12500, 256), jnp.float32)
        src = jax.random.randint(jax.random.fold_in(_gk, 2), (200000,), 0, 12500, jnp.int32)
        dst = jnp.minimum((12500 * jax.random.uniform(jax.random.fold_in(_gk, 3), (200000,)) ** 2.0).astype(jnp.int32), 99999)
        _o = jnp.argsort(dst, stable=True)
        src = src[_o]
        dst = dst[_o]
        edge_weight = jax.random.uniform(jax.random.fold_in(_gk, 12), (200000,), jnp.float32, 0.0, 0.999998)
        return (x, src, dst, edge_weight)
    x, src, dst, edge_weight = _rec_inputs()

    def _L0_gnn_setup():
        import jax, jax.numpy as jnp
        import numpy as np
        EPS = 1e-05

        def _bn(x, gamma, beta):
            m = jnp.mean(x, axis=0)
            v = jnp.mean((x - m) ** 2, axis=0)
            return gamma * (x - m) * jax.lax.rsqrt(v + EPS) + beta

        def _hconv(x, src, dst, ew, w1, b1, w2, b2, g, b):
            h = jax.nn.relu(x @ w1 + b1)
            msg = ew[:, None] * h[src]
            agg = jax.ops.segment_sum(msg, dst, num_segments=x.shape[0])
            h = agg @ w2 + b2
            return jax.nn.relu(_bn(h, g, b))
        N, C, E = (6250, 256, 37500)
        key = jax.random.key(seed)
        ks = jax.random.split(key, 16)
        s = 1.0 / np.sqrt(C)
        inp = {'x': jax.random.normal(ks[0], (N, C), dtype=jnp.float32), 'hyperedge_index': jax.random.randint(ks[1], (2, E), 0, N, dtype=jnp.int32), 'hyperedge_weight': jax.random.uniform(ks[2], (E,), dtype=jnp.float32), 'c1_w1': jax.random.normal(ks[3], (C, C), dtype=jnp.float32) * s, 'c1_b1': jnp.zeros((C,), jnp.float32), 'c1_w2': jax.random.normal(ks[4], (C, C), dtype=jnp.float32) * s, 'c1_b2': jnp.zeros((C,), jnp.float32), 'c1_g': jnp.ones((C,), jnp.float32), 'c1_b': jnp.zeros((C,), jnp.float32), 'bn1_g': jnp.ones((C,), jnp.float32), 'bn1_b': jnp.zeros((C,), jnp.float32), 'c2_w1': jax.random.normal(ks[5], (C, C), dtype=jnp.float32) * s, 'c2_b1': jnp.zeros((C,), jnp.float32), 'c2_w2': jax.random.normal(ks[6], (C, C), dtype=jnp.float32) * s, 'c2_b2': jnp.zeros((C,), jnp.float32), 'c2_g': jnp.ones((C,), jnp.float32), 'c2_b': jnp.zeros((C,), jnp.float32), 'bn2_g': jnp.ones((C,), jnp.float32), 'bn2_b': jnp.zeros((C,), jnp.float32)}
        return inp
    _L0_gnn_all = _L0_gnn_setup()
    _L0_gnn_in = {k: v for k, v in _L0_gnn_all.items() if k in ('c1_w1', 'c1_b1', 'c1_w2', 'c1_b2', 'c1_g', 'c1_b', 'bn1_g', 'bn1_b', 'c2_w1', 'c2_b1', 'c2_w2', 'c2_b2', 'c2_g', 'c2_b', 'bn2_g', 'bn2_b')}
    del _L0_gnn_all

    def _L0_ffn_setup():
        import jax, jax.numpy as jnp
        import numpy as np
        BN_EPS = 0.001

        def _bn(h, g, b, m, v):
            return g * (h - m) * jax.lax.rsqrt(v + BN_EPS) + b
        key = jax.random.key(seed)
        ks = jax.random.split(key, 8)
        B, F, Df = (256, 64, 256)
        E, H, D = (8, 256, 256)
        s1 = 1.0 / np.sqrt(Df)
        s2 = 1.0 / np.sqrt(H)
        return {'x': jax.random.normal(ks[0], (B, F, Df), jnp.float32), 'Wr': jax.random.normal(ks[1], (Df, E), jnp.float32) * s1, 'br': jnp.zeros((E,), jnp.float32), 'W1': jax.random.normal(ks[2], (E, Df, H), jnp.float32) * s1, 'b1': jnp.zeros((E, H), jnp.float32), 'g1': jnp.ones((E, H), jnp.float32), 'be1': jnp.zeros((E, H), jnp.float32), 'm1': jnp.zeros((E, H), jnp.float32), 'v1': jnp.ones((E, H), jnp.float32), 'W2': jax.random.normal(ks[3], (E, H, H), jnp.float32) * s2, 'b2': jnp.zeros((E, H), jnp.float32), 'g2': jnp.ones((E, H), jnp.float32), 'be2': jnp.zeros((E, H), jnp.float32), 'm2': jnp.zeros((E, H), jnp.float32), 'v2': jnp.ones((E, H), jnp.float32), 'Wo': jax.random.normal(ks[4], (E, H, D), jnp.float32) * s2, 'bo': jnp.zeros((E, D), jnp.float32)}
    _L0_ffn_all = _L0_ffn_setup()
    _L0_ffn_in = {k: v for k, v in _L0_ffn_all.items() if k in ('Wr', 'br', 'W1', 'b1', 'g1', 'be1', 'm1', 'v1', 'W2', 'b2', 'g2', 'be2', 'm2', 'v2', 'Wo', 'bo')}
    del _L0_ffn_all
    return {'x': x, 'src': src, 'dst': dst, 'edge_weight': edge_weight, 'L0_gnn_c1_w1': _L0_gnn_in['c1_w1'], 'L0_gnn_c1_b1': _L0_gnn_in['c1_b1'], 'L0_gnn_c1_w2': _L0_gnn_in['c1_w2'], 'L0_gnn_c1_b2': _L0_gnn_in['c1_b2'], 'L0_gnn_c1_g': _L0_gnn_in['c1_g'], 'L0_gnn_c1_b': _L0_gnn_in['c1_b'], 'L0_gnn_bn1_g': _L0_gnn_in['bn1_g'], 'L0_gnn_bn1_b': _L0_gnn_in['bn1_b'], 'L0_gnn_c2_w1': _L0_gnn_in['c2_w1'], 'L0_gnn_c2_b1': _L0_gnn_in['c2_b1'], 'L0_gnn_c2_w2': _L0_gnn_in['c2_w2'], 'L0_gnn_c2_b2': _L0_gnn_in['c2_b2'], 'L0_gnn_c2_g': _L0_gnn_in['c2_g'], 'L0_gnn_c2_b': _L0_gnn_in['c2_b'], 'L0_gnn_bn2_g': _L0_gnn_in['bn2_g'], 'L0_gnn_bn2_b': _L0_gnn_in['bn2_b'], 'L0_ffn_Wr': _L0_ffn_in['Wr'], 'L0_ffn_br': _L0_ffn_in['br'], 'L0_ffn_W1': _L0_ffn_in['W1'], 'L0_ffn_b1': _L0_ffn_in['b1'], 'L0_ffn_g1': _L0_ffn_in['g1'], 'L0_ffn_be1': _L0_ffn_in['be1'], 'L0_ffn_m1': _L0_ffn_in['m1'], 'L0_ffn_v1': _L0_ffn_in['v1'], 'L0_ffn_W2': _L0_ffn_in['W2'], 'L0_ffn_b2': _L0_ffn_in['b2'], 'L0_ffn_g2': _L0_ffn_in['g2'], 'L0_ffn_be2': _L0_ffn_in['be2'], 'L0_ffn_m2': _L0_ffn_in['m2'], 'L0_ffn_v2': _L0_ffn_in['v2'], 'L0_ffn_Wo': _L0_ffn_in['Wo'], 'L0_ffn_bo': _L0_ffn_in['bo']}

def reference(x, src, dst, edge_weight, L0_gnn_c1_w1, L0_gnn_c1_b1, L0_gnn_c1_w2, L0_gnn_c1_b2, L0_gnn_c1_g, L0_gnn_c1_b, L0_gnn_bn1_g, L0_gnn_bn1_b, L0_gnn_c2_w1, L0_gnn_c2_b1, L0_gnn_c2_w2, L0_gnn_c2_b2, L0_gnn_c2_g, L0_gnn_c2_b, L0_gnn_bn2_g, L0_gnn_bn2_b, L0_ffn_Wr, L0_ffn_br, L0_ffn_W1, L0_ffn_b1, L0_ffn_g1, L0_ffn_be1, L0_ffn_m1, L0_ffn_v1, L0_ffn_W2, L0_ffn_b2, L0_ffn_g2, L0_ffn_be2, L0_ffn_m2, L0_ffn_v2, L0_ffn_Wo, L0_ffn_bo):
    import jax
    import jax.numpy as jnp

    def _L0_gnn_ref(x, hyperedge_index, hyperedge_weight, c1_w1, c1_b1, c1_w2, c1_b2, c1_g, c1_b, bn1_g, bn1_b, c2_w1, c2_b1, c2_w2, c2_b2, c2_g, c2_b, bn2_g, bn2_b):
        import jax, jax.numpy as jnp
        import numpy as np
        EPS = 1e-05

        def _bn(x, gamma, beta):
            m = jnp.mean(x, axis=0)
            v = jnp.mean((x - m) ** 2, axis=0)
            return gamma * (x - m) * jax.lax.rsqrt(v + EPS) + beta

        def _hconv(x, src, dst, ew, w1, b1, w2, b2, g, b):
            h = jax.nn.relu(x @ w1 + b1)
            msg = ew[:, None] * h[src]
            agg = jax.ops.segment_sum(msg, dst, num_segments=x.shape[0])
            h = agg @ w2 + b2
            return jax.nn.relu(_bn(h, g, b))
        src, dst = (hyperedge_index[0], hyperedge_index[1])
        residual = x
        h = _hconv(x, src, dst, hyperedge_weight, c1_w1, c1_b1, c1_w2, c1_b2, c1_g, c1_b)
        h = jax.nn.relu(_bn(h, bn1_g, bn1_b))
        h = _hconv(h, src, dst, hyperedge_weight, c2_w1, c2_b1, c2_w2, c2_b2, c2_g, c2_b)
        h = _bn(h, bn2_g, bn2_b)
        return jax.nn.relu(h + residual)

    def _L0_ffn_ref(x, Wr, br, W1, b1, g1, be1, m1, v1, W2, b2, g2, be2, m2, v2, Wo, bo):
        import jax, jax.numpy as jnp
        import numpy as np
        BN_EPS = 0.001

        def _bn(h, g, b, m, v):
            return g * (h - m) * jax.lax.rsqrt(v + BN_EPS) + b
        feat = jnp.mean(x, axis=0)
        w = jax.nn.softmax(feat @ Wr + br, axis=-1)
        h = jnp.einsum('bfd,edh->bfeh', x, W1) + b1
        h = jax.nn.relu(_bn(h, g1, be1, m1, v1))
        h = jnp.einsum('bfeh,ehk->bfek', h, W2) + b2
        h = jax.nn.relu(_bn(h, g2, be2, m2, v2))
        y = jnp.einsum('bfeh,ehd->bfed', h, Wo) + bo
        return jnp.einsum('bfed,fe->bfd', y, w)
    edge_index = jnp.stack([src, dst])
    x = x + _L0_gnn_ref(_layernorm(x, axis=-1), edge_index, edge_weight, L0_gnn_c1_w1, L0_gnn_c1_b1, L0_gnn_c1_w2, L0_gnn_c1_b2, L0_gnn_c1_g, L0_gnn_c1_b, L0_gnn_bn1_g, L0_gnn_bn1_b, L0_gnn_c2_w1, L0_gnn_c2_b1, L0_gnn_c2_w2, L0_gnn_c2_b2, L0_gnn_c2_g, L0_gnn_c2_b, L0_gnn_bn2_g, L0_gnn_bn2_b)
    x = x + _L0_ffn_ref(_layernorm(x, axis=-1)[None], L0_ffn_Wr, L0_ffn_br, L0_ffn_W1, L0_ffn_b1, L0_ffn_g1, L0_ffn_be1, L0_ffn_m1, L0_ffn_v1, L0_ffn_W2, L0_ffn_b2, L0_ffn_g2, L0_ffn_be2, L0_ffn_m2, L0_ffn_v2, L0_ffn_Wo, L0_ffn_bo)[0]
    return x

_drawn_inputs = setup_inputs


def setup_inputs(seed=0):
    import zlib

    import numpy as np

    out = dict(_drawn_inputs(seed))
    spreads = {'L0_gnn_c1_b1': (0.0, 0.1),
     'L0_gnn_c1_b2': (0.0, 0.8),
     'L0_gnn_c1_g': (1.0, 0.6),
     'L0_gnn_c1_b': (0.0, 0.1),
     'L0_gnn_bn1_g': (1.0, 0.2),
     'L0_gnn_bn1_b': (0.0, 0.1),
     'L0_gnn_c2_b1': (0.0, 0.1),
     'L0_gnn_c2_b2': (0.0, 0.8),
     'L0_gnn_c2_g': (1.0, 0.6),
     'L0_gnn_c2_b': (0.0, 0.1),
     'L0_gnn_bn2_g': (1.0, 0.2),
     'L0_gnn_bn2_b': (0.0, 0.1),
     'L0_ffn_br': (0.0, 0.416),
     'L0_ffn_b1': (0.0, 0.561),
     'L0_ffn_g1': (1.0, 0.544),
     'L0_ffn_be1': (0.0, 0.572),
     'L0_ffn_m1': (0.0, 0.559),
     'L0_ffn_v1': (1.0, 0.6),
     'L0_ffn_b2': (0.0, 0.4),
     'L0_ffn_g2': (1.0, 0.2),
     'L0_ffn_be2': (0.0, 0.42),
     'L0_ffn_m2': (0.0, 0.415),
     'L0_ffn_v2': (1.0, 0.6),
     'L0_ffn_bo': (0.0, 0.3)}
    factors = {}
    for name, (base, spread) in spreads.items():
        noise = np.random.default_rng([zlib.crc32(name.encode()), seed]).standard_normal(out[name].shape)
        drawn = base * np.exp(spread * noise) if base else spread * noise
        out[name] = jnp.asarray(drawn.astype(out[name].dtype))
    for name, factor in factors.items():
        out[name] = (out[name] * factor).astype(out[name].dtype)
    return out
```

```python
def build(nc, a, out):
    import concourse.bass as bass
    from concourse import mybir
    from contextlib import ExitStack

    fp32, f32r, i32 = mybir.dt.float32, mybir.dt.float32r, mybir.dt.int32
    ALU, ACT, AX = mybir.AluOpType, mybir.ActivationFunctionType, mybir.AxisListType

    P = 128
    N, C = a["x"].shape
    E = a["src"].shape[0]
    NX = a["L0_ffn_Wr"].shape[1]
    KC = C // P
    TPC = 4
    CH = TPC * P
    NCH = -(-N // CH)
    ET = -(-E // P)
    EB = -(-ET // P)
    LN_EPS, BN_EPS, FFN_EPS = 1e-5, 1e-5, 1e-3
    assert C == KC * P and N > P and E > P

    def nodes(c):
        return min(CH, N - c * CH)

    def tiles(c):
        return [(j, min(P, nodes(c) - j * P)) for j in range(-(-nodes(c) // P))]

    def groups(c):
        full, rest = divmod(nodes(c), P)
        return ([(0, full, P)] if full else []) + ([(full, 1, rest)] if rest else [])

    top = ExitStack()

    class Stream:

        def __init__(self, name, by=1):
            self.sem, self.n, self.by = top.enter_context(nc.semaphore(name)), 0, by

    streams = {}

    def stream(name, by=1):
        if name not in streams:
            streams[name] = Stream(name, by)
        return streams[name]

    queues = {e: [] for e in ("sync", "scalar", "vector", "gpsimd", "tensor")}
    waited = {}

    def step(engine, signal, waits, fn):
        need = {}
        for w in waits:
            if w is not None:
                need[w[0]] = max(need.get(w[0], 0), w[1])
        todo = [(s, v) for s, v in need.items() if waited.get((engine, s), 0) < v]
        for s, v in todo:
            waited[(engine, s)] = v
        token = None
        if signal is not None:
            signal.n += signal.by
            token = (signal, signal.n)

        def emit(eng):
            for s, v in todo:
                eng.wait_ge(s.sem, v)
            ins = fn(eng)
            if signal is not None:
                ins.then_inc(signal.sem, signal.by)
        queues[engine].append(emit)
        return token

    entry = {
        "sync": lambda b: b.sync, "scalar": lambda b: b.scalar, "vector": lambda b: b.vector,
        "gpsimd": lambda b: b.gpsimd, "tensor": lambda b: b.tensor,
    }

    def run_block():
        with nc.Block() as block:
            for name in queues:
                def body(eng, todo=list(queues[name])):
                    for emit in todo:
                        emit(eng)
                entry[name](block)(body)
                queues[name].clear()

    def dma(engine, name, waits, dst, src):
        return step(engine, stream(name, 16), waits, lambda g: g.dma_start(dst, src))

    def dve(name, waits, fn):
        return step("vector", stream(name), waits, fn)

    def act(name, waits, fn):
        return step("scalar", stream(name), waits, fn)

    def pool(name, waits, fn):
        return step("gpsimd", stream(name), waits, fn)

    def pe(name, waits, fns):
        def emit(g):
            for f in fns:
                ins = f(g)
            return ins
        return step("tensor", stream(name), waits, emit)

    def mm(o, l, r, start, stop):
        return lambda g: nc.tensor.matmul(o, l, r, start=start, stop=stop)

    def tr(o, i, ident_rows):
        return lambda g: nc.tensor.transpose(o, i, ident_rows)

    def rows_of(dram, c, buf, write):
        for j, k, r in groups(c):
            lo = c * CH + j * P
            d = dram[lo:lo + k * r, :].rearrange("(k p) n -> p k n", p=r)
            s = buf[0:r, j:j + k, :]
            yield (d, s) if write else (s, d)

    with top:
        def sb(ctx, name, shape, dt=fp32):
            return ctx.enter_context(nc.sbuf_tensor(name, shape, dt))

        def ps(ctx, name, shape):
            return ctx.enter_context(nc.psum_tensor(name, shape, fp32))

        h_dram = [nc.dram_tensor(f"h{i}", (N, C), fp32, kind="Internal").ap() for i in range(2)]
        x1_dram = nc.dram_tensor("x1", (N, C), fp32, kind="Internal").ap()
        base_dram = nc.dram_tensor("tile_base", (EB, P), i32, kind="Internal").ap()

        ident = sb(top, "ident", [P, P])
        eps_ln = sb(top, "eps_ln", [P, 1])
        eps_ffn = sb(top, "eps_ffn", [P, 1])
        ones_row = sb(top, "ones_row", [1, P])
        ln1 = sb(top, "ln1", [P, NCH * TPC, 2])
        conv_p = sb(top, "conv_p", [P, 10 * KC])
        ffn_p = [sb(top, f"ffn_p{i}", [P, 5 * NX * KC]) for i in range(2)]
        wr_raw = sb(top, "wr_raw", [P, KC, NX])
        br_all = sb(top, "br_all", [P, NX])
        bo_sb = sb(top, "bo_sb", [NX, C])

        conv_names = [f"L0_gnn_{n}" for c in "12" for n in (f"c{c}_b2", f"c{c}_g", f"c{c}_b", f"bn{c}_g", f"bn{c}_b")]

        def conv_col(layer, which, m):
            i = KC * (5 * layer + which) + m
            return conv_p[:, i:i + 1]

        def conv_cols(layer, which):
            i = KC * (5 * layer + which)
            return conv_p[:, i:i + KC]

        convs = ExitStack()
        w1 = [sb(convs, f"w1_{i}", [P, KC, C]) for i in range(2)]
        w2 = [sb(convs, f"w2_{i}", [P, KC, C]) for i in range(2)]
        b1_all = [sb(convs, f"b1_{i}", [P, C]) for i in range(2)]
        AW = N + P
        agg = sb(convs, "agg", [P, KC, AW])
        edges = ExitStack()
        src_col = sb(edges, "src_col", [P, EB * P], i32)
        rel_col = sb(edges, "rel_col", [P, EB * P])
        ew_col = sb(edges, "ew_col", [P, EB * P])
        base_row = sb(edges, "base_row", [1, EB * P], i32)
        lane = sb(edges, "lane", [P, P])
        far = sb(edges, "far", [1, 1], i32)

        with ExitStack() as s:
            raw = {n: sb(s, f"{n}_raw", [P, EB, P], dt) for n, dt in (("src", i32), ("dst", i32), ("ew", fp32))}
            src_f = sb(s, "src_f", [P, EB, P])
            dst_f = sb(s, "dst_f", [P, EB, P])
            tile_min = sb(s, "tile_min", [P, EB])
            tile_max = sb(s, "tile_max", [P, EB])
            span = sb(s, "span", [P, 1])
            base_i = sb(s, "base_i", [EB, P], i32)
            prow = [sb(s, f"prow{i}", [P, P]) for i in range(3)]
            brow = sb(s, "brow", [1, 2 * C + NX])
            pt = [ps(s, f"pt{i}", [P, 512]) for i in range(4)]

            zi = pool("init", [], lambda g: g.memset(ident[:, :], 0.0))
            ident_ready = pool("init", [zi], lambda g: g.affine_select(
                out=ident[:, :], in_=ident[:, :], compare_op=ALU.not_equal, fill=1.0, base=0,
                pattern=[[-1, P]], channel_multiplier=1))
            pool("init", [], lambda g: g.memset(eps_ln[:, :], LN_EPS))
            pool("init", [], lambda g: g.memset(eps_ffn[:, :], FFN_EPS))
            ones_ready = pool("init", [], lambda g: g.memset(ones_row[:, :], 1.0))
            pool("init", [], lambda g: g.iota(lane[:, :], pattern=[[1, P]], base=0, channel_multiplier=0,
                                              allow_small_or_imprecise_dtypes=True))
            agg_zero = pool("init", [], lambda g: g.memset(agg[:, :, :], 0.0))

            clear = [dve("clear", [], lambda g, r=r: g.memset(r[:, EB - 1, :], 0)) for r in raw.values()]
            loaded = {}
            full_blocks, last_tiles, last_edges = ET // P, (E - (ET // P) * P * P) // P, E % P
            for n, dram in (("src", a["src"]), ("dst", a["dst"]), ("ew", a["edge_weight"])):
                lo = full_blocks * P * P
                t = [dma("sync", f"ld_{n}", [], raw[n][:, 0:full_blocks, :],
                         dram[0:lo].rearrange("(b p e) -> p b e", p=P, e=P))]
                if last_tiles:
                    t.append(dma("sync", f"ld_{n}", [clear[-1]], raw[n][0:last_tiles, EB - 1, :],
                                 dram[lo:lo + last_tiles * P].rearrange("(p e) -> p e", e=P)))
                if last_edges:
                    lo += last_tiles * P
                    tail = dram[lo:E].rearrange("(p e) -> p e", p=1)
                    t.append(dma("sync", f"ld_{n}", [clear[-1]],
                                 raw[n][last_tiles:last_tiles + 1, EB - 1, 0:last_edges], tail))
                    if n == "dst":
                        need = P - last_edges
                        t.append(dma("sync", f"ld_{n}", [],
                                     raw[n][last_tiles:last_tiles + 1, EB - 1, last_edges:P],
                                     dram[E - need:E].rearrange("(p e) -> p e", p=1)))
                loaded[n] = t[-1]

            t = None
            for layer in range(2):
                for w, n in ((w1, "w1"), (w2, "w2")):
                    dma("scalar", "ld_w", [], w[layer][:, :, :],
                        a[f"L0_gnn_c{layer + 1}_{n}"].rearrange("(k p) n -> p k n", p=P))
                t = dma("scalar", "ld_par", [], brow[0:1, layer * C:(layer + 1) * C],
                        a[f"L0_gnn_c{layer + 1}_b1"].rearrange("(p n) -> p n", p=1))
            dma("scalar", "ld_par", [], brow[0:1, 2 * C:2 * C + NX], a["L0_ffn_br"].rearrange("(p n) -> p n", p=1))
            dma("scalar", "ld_par", [], bo_sb[:, :], a["L0_ffn_bo"])
            dma("scalar", "ld_par", [], wr_raw[:, :, :], a["L0_ffn_Wr"].rearrange("(k p) n -> p k n", p=P))
            for i, n in enumerate(conv_names):
                dma("scalar", "ld_par", [], prow[2][KC * i:KC * (i + 1), :], a[n].rearrange("(m p) -> m p", p=P))
            for layer in range(2):
                for i, n in enumerate(("g", "b", "be", "m", "v")):
                    w = NX * KC
                    params = dma("scalar", "ld_par", [], prow[layer][w * i:w * (i + 1), :],
                                 a[f"L0_ffn_{n}{layer + 1}"].rearrange("e (m p) -> (e m) p", p=P))
            weights_loaded = (stream("ld_w"), stream("ld_w").n)

            pars = []
            for i, (dst, w) in enumerate(((ffn_p[0], 5 * NX * KC), (ffn_p[1], 5 * NX * KC), (conv_p, 10 * KC))):
                turned = pe("p_par", [params, ident_ready], [tr(pt[i][:, 0:w], prow[i][0:w, :], ident[0:w, 0:w])])
                pars.append(dve("v_par", [turned], lambda g, dst=dst, i=i, w=w: g.tensor_copy(dst[:, :], pt[i][:, 0:w])))
            for i, (dst, lo, w) in enumerate(((b1_all[0], 0, C), (b1_all[1], C, C), (br_all, 2 * C, NX))):
                spread = pe("p_par", [ones_ready, pars[i]],
                            [mm(pt[i][:, 0:w], ones_row[:, :], brow[0:1, lo:lo + w], True, True)])
                par_done = dve("v_par", [spread], lambda g, dst=dst, i=i, w=w: g.tensor_copy(dst[:, :], pt[i][:, 0:w]))

            c_src = dve("v_idx", [loaded["src"], clear[-1]], lambda g: g.tensor_copy(src_f[:, :, :], raw["src"][:, :, :]))
            c_dst = dve("v_idx", [loaded["dst"], clear[-1]], lambda g: g.tensor_copy(dst_f[:, :, :], raw["dst"][:, :, :]))
            t_min = dve("v_idx", [c_dst], lambda g: g.tensor_reduce(tile_min[:, :], dst_f[:, :, :], AX.X, ALU.min))
            m = dve("v_idx", [c_dst], lambda g: g.tensor_reduce(tile_max[:, :], dst_f[:, :, :], AX.X, ALU.max))
            m = dve("v_idx", [m, t_min], lambda g: g.tensor_tensor(tile_max[:, :], tile_max[:, :], tile_min[:, :], ALU.subtract))
            m = dve("v_idx", [m], lambda g: g.tensor_reduce(span[:, :], tile_max[:, :], AX.X, ALU.max))
            m = pe("p_idx", [m, ident_ready, par_done], [tr(pt[3][0:1, 0:P], span[:, :], ident[:, :])])
            m = dve("v_idx", [m], lambda g: g.tensor_reduce(span[0:1, :], pt[3][0:1, 0:P], AX.X, ALU.max))
            m = dve("v_idx", [m], lambda g: g.tensor_copy(far[:, :], span[0:1, :]))
            m = dve("v_idx", [m], lambda g: g.tensor_single_scalar(far[:, :], far[:, :], P.bit_length() - 1, ALU.arith_shift_right))
            for b in range(EB):
                rel = dve("v_idx", [t_min], lambda g, b=b: g.tensor_scalar(
                    dst_f[:, b, :], dst_f[:, b, :], tile_min[:, b:b + 1], None, ALU.subtract))
            tb = pe("p_idx", [t_min, ident_ready, m], [tr(pt[3][0:EB, 0:P], tile_min[:, :], ident[:, :])])
            base_ready = dve("v_idx", [tb], lambda g: g.tensor_copy(base_i[:, :], pt[3][0:EB, 0:P]))
            stored = dma("sync", "st_base", [base_ready], base_dram, base_i[:, :])
            base_loaded = dma("sync", "ld_base", [stored], base_row[:, :],
                              base_dram.rearrange("(o b) p -> o (b p)", o=1))
            freed = [par_done, par_done, par_done, base_ready]
            n = 0
            for srcbuf, dstbuf, ready in ((src_f, src_col, c_src), (raw["ew"], ew_col, loaded["ew"]), (dst_f, rel_col, rel)):
                for b in range(0, EB, 4):
                    k = min(4, EB - b)
                    q = n % 4
                    turned = pe("p_idx", [ready, freed[q]],
                                [tr(pt[q][:, i * P:(i + 1) * P], srcbuf[:, b + i, :], ident[:, :]) for i in range(k)])
                    f = lambda g, dstbuf=dstbuf, b=b, k=k, q=q: g.tensor_copy(
                        dstbuf[:, b * P:(b + k) * P], pt[q][:, 0:k * P])
                    freed[q] = dve("v_idx", [turned], f)
                    n += 1
            dve("seen", [base_loaded, weights_loaded, params], lambda g: g.memset(base_i[0:1, 0:1], 0))
            run_block()

        def row_stats(tag, c, x, stats, mv, waits):
            for j, r in tiles(c):
                t = dve(f"{tag}_st", waits, lambda g, j=j, r=r: g.bn_stats(stats[0:r, j, :], x[0:r, j, :]))
            for j, r in tiles(c):
                t2 = dve(f"{tag}_ag", [t], lambda g, j=j, r=r: g.bn_aggr(mv[0:r, j, :], stats[0:r, j, :]))
            for j, k, r in groups(c):
                t3 = act(f"{tag}_sd", [t2], lambda g, j=j, k=k, r=r: g.activation(
                    mv[0:r, j:j + k, 1], mv[0:r, j:j + k, 1], ACT.Sqrt, bias=eps_ln[0:r, :]))
            for j, k, r in groups(c):
                t4 = dve(f"{tag}_rs", [t3], lambda g, j=j, k=k, r=r: g.reciprocal(
                    mv[0:r, j:j + k, 1], mv[0:r, j:j + k, 1]))
            return t4

        def normalize(tag, c, dst, x, mv, waits):
            for j, r in tiles(c):
                t = dve(f"{tag}_nm", waits, lambda g, j=j, r=r: g.tensor_scalar(
                    dst[0:r, j, :], x[0:r, j, :], mv[0:r, j, 0:1], mv[0:r, j, 1:2], ALU.subtract, ALU.mult))
            return t

        def hidden_rows(tag, c, colsT, w, bias, hbuf, pH, h_out, col_ready, pH_free, hbuf_free):
            prod = pe(f"{tag}_h", [col_ready, pH_free],
                      [mm(pH[0:r, j, :], colsT[:, k, j * P:j * P + r], w[:, k, :], k == 0, k == KC - 1)
                       for j, r in tiles(c) for k in range(KC)])
            for j, k, r in groups(c):
                biased = dve(f"{tag}_hb", [prod, hbuf_free], lambda g, j=j, k=k, r=r: g.tensor_tensor(
                    hbuf[0:r, j:j + k, :], pH[0:r, j:j + k, :],
                    bias[0:r, :].unsqueeze(1).broadcast_to([r, k, C]), ALU.add))
            for j, k, r in groups(c):
                relu = act(f"{tag}_hr", [biased], lambda g, j=j, k=k, r=r: g.activation(
                    hbuf[0:r, j:j + k, :], hbuf[0:r, j:j + k, :], ACT.Relu))
            for d, sbuf in rows_of(h_out, c, hbuf, True):
                st = dma("sync", f"{tag}_hst{c % 2}", [relu], d, sbuf)
            return prod, biased, st

        with ExitStack() as s:
            X = [sb(s, f"a_x{i}", [P, TPC, C]) for i in range(2)]
            Y = [sb(s, f"a_y{i}", [P, TPC, C]) for i in range(2)]
            YT = [sb(s, f"a_yt{i}", [P, KC, CH]) for i in range(2)]
            H = [sb(s, f"a_h{i}", [P, TPC, C]) for i in range(2)]
            ST = [sb(s, f"a_st{i}", [P, TPC, 6]) for i in range(2)]
            pT = [ps(s, f"a_pt{i}", [P, KC, CH]) for i in range(2)]
            pH = [ps(s, f"a_ph{i}", [P, TPC, C]) for i in range(2)]
            normed, turned, evac, prod, biased, hst = {}, {}, {}, {}, {}, {}
            front, back = [], []
            for c in range(NCH + 1):
                if c < NCH:
                    b = c % 2
                    mv = ln1[:, c * TPC:(c + 1) * TPC, :]
                    for d, sbuf in rows_of(a["x"], c, X[b], False):
                        ld = dma("sync", f"a_ld{b}", [normed.get(c - 2)], d, sbuf)
                    rs = row_stats("a", c, X[b], ST[b], mv, [ld])
                    normed[c] = normalize("a", c, Y[b], X[b], mv, [rs, turned.get(c - 2)])
                    turned[c] = pe("a_t", [normed[c], evac.get(c - 2)],
                                   [tr(pT[b][:, k, j * P:j * P + r], Y[b][0:r, j, k * P:(k + 1) * P], ident[0:r, 0:r])
                                    for j, r in tiles(c) for k in range(KC)])
                    nn = nodes(c)
                    evac[c] = act("a_ev", [turned[c], prod.get(c - 2)], lambda g, b=b, nn=nn: g.activation(
                        YT[b][:, :, 0:nn], pT[b][:, :, 0:nn], ACT.Copy))
                if c >= 1:
                    q = c - 1
                    prod[q], biased[q], hst[q] = hidden_rows(
                        "a", q, YT[q % 2], w1[0], b1_all[0], H[q % 2], pH[q % 2], h_dram[0],
                        evac[q], biased.get(q - 2), hst.get(q - 2))
            step("sync", stream("fence"), [hst[NCH - 1], hst[NCH - 2]], lambda g: g.nop())
            run_block()

        def aggregate(layer):
            R, RO, RP = 10, 4, 4
            with ExitStack() as s:
                G = [sb(s, f"g{layer}_{i}", [P, C]) for i in range(R)]
                OH = [sb(s, f"oh{layer}_{i}", [P, P]) for i in range(RO)]
                pA = [ps(s, f"pa{layer}_{i}", [P, 512]) for i in range(RP)]
                sums, onehot, added = {}, {}, {}
                t = f"g{layer}"
                LAG = 2
                regs = {}
                BATCH = 16

                def load_bases(g, e):
                    if not regs:
                        regs["r"] = [g.alloc_register(f"{t}_base{i}") for i in range(BATCH)]
                    k = min(BATCH, ET - e)
                    return g.load(regs["r"][0:k], base_row[0:1, e:e + k])

                for e in range(ET + LAG):
                    if e < ET:
                        gathered = step("gpsimd", stream(f"{t}_ga{e % R}", 16), [sums.get(e - R)],
                                        lambda g, e=e: g.indirect_dma_start(
                                            G[e % R][:, :], None, h_dram[layer],
                                            bass.IndirectOffsetOnAxis(ap=src_col[:, e:e + 1], axis=0)))
                        onehot[e] = dve(f"{t}_oh", [sums.get(e - RO)], lambda g, e=e: g.tensor_scalar(
                            OH[e % RO][:, :], lane[:, :], rel_col[:, e:e + 1], ew_col[:, e:e + 1],
                            ALU.is_equal, ALU.mult))
                        sums[e] = pe(f"{t}_mm", [gathered, onehot[e], added.get(e - RP)],
                                     [mm(pA[e % RP][:, k * P:(k + 1) * P], G[e % R][:, k * P:(k + 1) * P],
                                         OH[e % RO][:, :], True, True) for k in range(KC)])
                    if e >= LAG:
                        q = e - LAG

                        def add(g, q=q):
                            if q % BATCH == 0:
                                load_bases(g, q)
                            base = g.snap(regs["r"][q % BATCH], min_val=0, max_val=N - 1)
                            win = agg[:, :, bass.ds(base, P)]
                            return g.tensor_tensor(win, win, pA[q % RP][:, 0:KC * P].rearrange(
                                "p (k n) -> p k n", k=KC), ALU.add)
                        added[q] = dve(f"{t}_add", [sums[q], added.get(q - 1)], add)
                far_windows(layer, s, G[0], OH[0], pA[0])
                run_block()

        def far_windows(layer, s, G, OH, pA):
            t = f"x{layer}"
            idx = sb(s, f"{t}_idx", [P, 1], i32)
            rel_w = sb(s, f"{t}_rel", [P, EB * P])
            rel_e, ew_e = sb(s, f"{t}_rel_e", [P, 1]), sb(s, f"{t}_ew_e", [P, 1])
            base_f = sb(s, f"{t}_base_f", [1, EB * P])
            base_w = sb(s, f"{t}_base_w", [1, EB * P], i32)
            sem = {n: top.enter_context(nc.semaphore(f"{t}_{n}"))
                   for n in ("idx", "gathered", "landed", "onehot", "sums", "added", "fixed", "turn")}

            def take(g, name):
                g.wait_ge(sem[name], 1)
                g.sem_clear(sem[name])

            def loops(g):
                count = g.alloc_register(f"{t}_far")
                g.load(count, far[0:1, 0:1])
                return count

            def pool_loop(g):
                count = loops(g)
                with g.If_ne(count, 0):
                    with g.Fori(0, count):
                        with g.Fori(0, ET) as e:
                            g.tensor_copy(idx[:, :], src_col[:, bass.ds(e, 1)]).then_inc(sem["idx"], 1)
                            take(g, "idx")
                            g.indirect_dma_start(G[:, :], None, h_dram[layer], bass.IndirectOffsetOnAxis(
                                ap=idx[:, :], axis=0)).then_inc(sem["gathered"], 16)
                            g.wait_ge(sem["gathered"], 16)
                            g.dma_reset(range(sem["gathered"].num, sem["gathered"].num + 1))
                            g.sem_clear(sem["gathered"])
                            g.sem_inc(sem["landed"], 1)
                            take(g, "added")
                return g.nop()

            def pe_loop(g):
                count = loops(g)
                with g.If_ne(count, 0):
                    with g.Fori(0, count):
                        with g.Fori(0, ET):
                            take(g, "landed")
                            take(g, "onehot")
                            for k in range(KC):
                                ins = nc.tensor.matmul(pA[:, k * P:(k + 1) * P], G[:, k * P:(k + 1) * P], OH[:, :],
                                                       start=True, stop=True)
                            ins.then_inc(sem["sums"], 1)
                return g.nop()

            def dve_loop(g):
                def done(ins):
                    ins.then_inc(sem["fixed"], 1)
                    take(g, "fixed")

                count = loops(g)
                with g.If_ne(count, 0):
                    done(g.tensor_copy(rel_w[:, :], rel_col[:, :]))
                    done(g.tensor_copy(base_f[:, :], base_row[:, :]))
                    with g.Fori(0, count):
                        done(g.tensor_scalar(rel_w[:, :], rel_w[:, :], float(P), None, ALU.subtract))
                        done(g.tensor_scalar(base_f[:, :], base_f[:, :], float(P), float(N), ALU.add, ALU.min))
                        done(g.tensor_copy(base_w[:, :], base_f[:, :]))
                        with g.Fori(0, ET) as e:
                            done(g.tensor_copy(rel_e[:, :], rel_w[:, bass.ds(e, 1)]))
                            done(g.tensor_copy(ew_e[:, :], ew_col[:, bass.ds(e, 1)]))
                            g.tensor_scalar(OH[:, :], lane[:, :], rel_e[:, :], ew_e[:, :], ALU.is_equal,
                                            ALU.mult).then_inc(sem["onehot"], 1)
                            base = g.value_load(base_w[0:1, bass.ds(e, 1)], min_val=0, max_val=N)
                            take(g, "sums")
                            win = agg[:, :, bass.ds(base, P)]
                            g.tensor_tensor(win, win, pA[:, 0:KC * P].rearrange("p (k n) -> p k n", k=KC),
                                            ALU.add).then_inc(sem["turn"], 1)
                            take(g, "turn")
                            g.sem_inc(sem["added"], 1)
                return g.nop()

            last_add, last_sum = stream(f"g{layer}_add"), stream(f"g{layer}_mm")
            done_add, done_sum = (last_add, last_add.n), (last_sum, last_sum.n)
            step("gpsimd", None, [done_sum], pool_loop)
            step("vector", None, [done_add, done_sum], dve_loop)
            step("tensor", None, [done_add], pe_loop)

        def norm_terms(tag, layer, which, stats, scale, shift, waits):
            mv = tag_mv[tag]
            for m in range(KC):
                t = dve("bn_ag", waits, lambda g, m=m: g.bn_aggr(
                    mv[:, m, :], stats[:, m, :, :].rearrange("p c s -> p (c s)")))
            t = act("bn_sd", [t], lambda g: g.activation(mv[:, :, 1], mv[:, :, 1], ACT.Sqrt, bias=eps_ln[:, :]))
            t = dve("bn_tm", [t], lambda g: g.reciprocal(mv[:, :, 1], mv[:, :, 1]))
            t = dve("bn_tm", [t], lambda g: g.tensor_tensor(scale[:, :], mv[:, :, 1], conv_cols(layer, which), ALU.mult))
            t = dve("bn_tm", [t], lambda g: g.tensor_tensor(mv[:, :, 0], mv[:, :, 0], scale[:, :], ALU.mult))
            return dve("bn_tm", [t], lambda g: g.tensor_tensor(shift[:, :], conv_cols(layer, which + 1), mv[:, :, 0], ALU.subtract))

        tag_mv = {}

        def conv_tail(layer, s, sc2, sh2):
            t = f"c{layer}"
            pZ = [ps(s, f"{t}_pz{i}", [P, KC, CH]) for i in range(2)]
            stats = [sb(s, f"{t}_st{i}", [P, KC, NCH, 6]) for i in range(2)]
            for i in range(2):
                tag_mv[f"{t}{i}"] = sb(s, f"{t}_mv{i}", [P, KC, 2])
            sc1, sh1 = sb(s, f"{t}_sc1", [P, KC]), sb(s, f"{t}_sh1", [P, KC])
            ev, st = {}, None
            for c in range(NCH):
                nn, lo = nodes(c), c * CH
                prod = pe(f"{t}_z", [ev.get(c - 2)],
                          [mm(pZ[c % 2][:, m, 0:nn], w2[layer][:, k, m * P:(m + 1) * P], agg[:, k, lo:lo + nn],
                              k == 0, k == KC - 1) for m in range(KC) for k in range(KC)])
                for m in range(KC):
                    ev[c] = act(f"{t}_ze", [prod], lambda g, m=m, nn=nn, lo=lo, c=c: g.activation(
                        agg[:, m, lo:lo + nn], pZ[c % 2][:, m, 0:nn], ACT.Identity, bias=conv_col(layer, 0, m)))
                for m in range(KC):
                    st = dve(f"{t}_zs", [ev[c]], lambda g, m=m, nn=nn, lo=lo, c=c: g.bn_stats(
                        stats[0][:, m, c, :], agg[:, m, lo:lo + nn]))
            terms = norm_terms(f"{t}0", layer, 1, stats[0], sc1, sh1, [st])
            for c in range(NCH):
                nn, lo = nodes(c), c * CH
                for m in range(KC):
                    u = act(f"{t}_u", [terms], lambda g, m=m, nn=nn, lo=lo: g.activation(
                        agg[:, m, lo:lo + nn], agg[:, m, lo:lo + nn], ACT.Relu, bias=sh1[:, m:m + 1],
                        scale=sc1[:, m:m + 1]))
                    st = dve(f"{t}_us", [u], lambda g, m=m, nn=nn, lo=lo, c=c: g.bn_stats(
                        stats[1][:, m, c, :], agg[:, m, lo:lo + nn]))
            return norm_terms(f"{t}1", layer, 3, stats[1], sc2, sh2, [st])

        aggregate(0)
        with ExitStack() as s:
            sc2, sh2 = sb(s, "b_sc2", [P, KC]), sb(s, "b_sh2", [P, KC])
            VT = [sb(s, f"b_v{i}", [P, KC, CH]) for i in range(2)]
            H = [sb(s, f"b_h{i}", [P, TPC, C]) for i in range(2)]
            pH = [ps(s, f"b_ph{i}", [P, TPC, C]) for i in range(2)]
            terms = conv_tail(0, s, sc2, sh2)
            prod, biased, hst, vt = {}, {}, {}, {}
            for c in range(NCH + 1):
                if c < NCH:
                    nn, lo, b = nodes(c), c * CH, c % 2
                    for m in range(KC):
                        vt[c] = act("b_v", [terms, prod.get(c - 2)], lambda g, m=m, nn=nn, lo=lo, b=b: g.activation(
                            VT[b][:, m, 0:nn], agg[:, m, lo:lo + nn], ACT.Relu, bias=sh2[:, m:m + 1],
                            scale=sc2[:, m:m + 1]))
                    pool("b_clr", [vt[c]], lambda g, lo=lo, nn=nn, c=c: g.memset(
                        agg[:, :, lo:(lo + nn if c < NCH - 1 else AW)], 0.0))
                if c >= 1:
                    q = c - 1
                    prod[q], biased[q], hst[q] = hidden_rows(
                        "b", q, VT[q % 2], w1[1], b1_all[1], H[q % 2], pH[q % 2], h_dram[1],
                        vt[q], biased.get(q - 2), hst.get(q - 2))
            step("sync", stream("fence"), [hst[NCH - 1], hst[NCH - 2]], lambda g: g.nop())
            run_block()

        aggregate(1)
        edges.close()
        with ExitStack() as s:
            sc2, sh2 = sb(s, "d_sc2", [P, KC]), sb(s, "d_sh2", [P, KC])
            QT = [sb(s, f"d_q{i}", [P, KC, CH]) for i in range(2)]
            X = [sb(s, f"d_x{i}", [P, TPC, C]) for i in range(2)]
            Y = [sb(s, f"d_y{i}", [P, TPC, C]) for i in range(2)]
            pR = [ps(s, f"d_pr{i}", [P, TPC, C]) for i in range(2)]
            terms = conv_tail(1, s, sc2, sh2)
            turned, summed, stored = {}, {}, {}
            for c in range(NCH):
                nn, lo, b = nodes(c), c * CH, c % 2
                mv = ln1[:, c * TPC:(c + 1) * TPC, :]
                for d, sbuf in rows_of(a["x"], c, X[b], False):
                    ld = dma("sync", f"d_ld{b}", [summed.get(c - 2)], d, sbuf)
                for m in range(KC):
                    q = act("d_q", [terms, turned.get(c - 2)], lambda g, m=m, nn=nn, lo=lo, b=b: g.activation(
                        QT[b][:, m, 0:nn], agg[:, m, lo:lo + nn], ACT.Identity, bias=sh2[:, m:m + 1],
                        scale=sc2[:, m:m + 1]))
                turned[c] = pe("d_t", [q, summed.get(c - 2)],
                               [tr(pR[b][0:r, j, k * P:(k + 1) * P], QT[b][:, k, j * P:j * P + r], ident[:, :])
                                for j, r in tiles(c) for k in range(KC)])
                nm = normalize("d", c, Y[b], X[b], mv, [ld, stored.get(c - 2)])
                for j, k, r in groups(c):
                    a1 = dve("d_a", [nm, turned[c]], lambda g, j=j, k=k, r=r, b=b: g.tensor_tensor(
                        Y[b][0:r, j:j + k, :], pR[b][0:r, j:j + k, :], Y[b][0:r, j:j + k, :], ALU.add))
                for j, k, r in groups(c):
                    summed[c] = dve("d_s", [a1], lambda g, j=j, k=k, r=r, b=b: g.scalar_tensor_tensor(
                        Y[b][0:r, j:j + k, :], Y[b][0:r, j:j + k, :], 0.0, X[b][0:r, j:j + k, :], ALU.max, ALU.add))
                for d, sbuf in rows_of(x1_dram, c, Y[b], True):
                    stored[c] = dma("scalar", f"d_st{b}", [summed[c]], d, sbuf)
            step("sync", stream("fence"), [stored[NCH - 1], stored[NCH - 2]], lambda g: g.nop())
            run_block()
        convs.close()

        with ExitStack() as s:
            names = ("W1", "W2", "Wo")
            whi = {n: sb(s, f"{n}_hi", [P, NX, KC, C], f32r) for n in names}
            wlo = {n: sb(s, f"{n}_lo", [P, NX, KC, C], f32r) for n in names}
            wst = [sb(s, f"wst{i}", [P, KC, C]) for i in range(2)]
            wrh, wrl = sb(s, "wrh", [P, KC, NX], f32r), sb(s, "wrl", [P, KC, NX], f32r)
            scale = [sb(s, f"f_sc{i}", [P, NX * KC]) for i in range(2)]
            shift = [sb(s, f"f_sh{i}", [P, NX * KC]) for i in range(2)]
            x1 = [sb(s, f"f_x{i}", [P, TPC, C]) for i in range(2)]
            y = sb(s, "f_y", [P, TPC, C])
            yhi = [sb(s, f"f_yh{i}", [P, KC, CH], f32r) for i in range(2)]
            ylo = [sb(s, f"f_yl{i}", [P, KC, CH], f32r) for i in range(2)]
            hf = [sb(s, f"f_hf{i}", [P, KC, CH]) for i in range(2)]
            hhi = [[sb(s, f"f_hh{l}{i}", [P, KC, CH], f32r) for i in range(2)] for l in range(2)]
            hlo = [[sb(s, f"f_hl{l}{i}", [P, KC, CH], f32r) for i in range(2)] for l in range(2)]
            ST = sb(s, "f_st", [P, TPC, 6])
            MV = sb(s, "f_mv", [P, TPC, 2])
            lg = sb(s, "f_lg", [P, TPC, NX])
            ex = sb(s, "f_ex", [P, TPC, NX])
            mx = sb(s, "f_mx", [P, TPC])
            sm = sb(s, "f_sm", [P, TPC])
            gate = [sb(s, f"f_gate{i}", [P, TPC, NX]) for i in range(2)]
            gT = sb(s, "f_gt", [NX, CH])
            p1 = ps(s, "f_p1", [P, KC, CH])
            p2 = ps(s, "f_p2", [P, KC, CH])
            p3 = ps(s, "f_p3", [P, TPC, C])
            pm = ps(s, "f_pm", [P, KC * CH])

            for l in range(2):
                w = NX * KC
                g_, b_, be_, m_, v_ = (ffn_p[l][:, i * w:(i + 1) * w] for i in range(5))
                t = act("f_sd", [], lambda g, v_=v_: g.activation(v_, v_, ACT.Sqrt, bias=eps_ffn[:, :]))
                t = dve("f_tm", [t], lambda g, v_=v_: g.reciprocal(v_, v_))
                t = dve("f_tm", [t], lambda g, v_=v_, g_=g_, l=l: g.tensor_tensor(scale[l][:, :], v_, g_, ALU.mult))
                t1 = dve("f_tm", [], lambda g, b_=b_, m_=m_: g.tensor_tensor(b_, b_, m_, ALU.subtract))
                t = dve("f_tm", [t1], lambda g, b_=b_, l=l: g.tensor_tensor(b_, b_, scale[l][:, :], ALU.mult))
                terms = dve("f_tm", [t], lambda g, b_=b_, be_=be_, l=l: g.tensor_tensor(shift[l][:, :], b_, be_, ALU.add))
            t = act("f_wr", [], lambda g: g.activation(wrh[:, :, :], wr_raw[:, :, :], ACT.Copy))
            wr_ready = dve("f_wl", [t], lambda g: g.tensor_tensor(
                wrl[:, :, :], wr_raw[:, :, :], wrh[:, :, :].bitcast(fp32), ALU.subtract))

            w_ready, w_n = {}, 0
            w_split = {}

            def split_weight(n, e):
                i = len(w_ready)
                b = i % 2
                ld = dma("sync", f"f_wld{b}", [w_split.get(i - 2)], wst[b][:, :, :],
                         a[f"L0_ffn_{n}"][e].rearrange("(k p) n -> p k n", p=P))
                hi = act("f_wh", [ld], lambda g: g.activation(whi[n][:, e, :, :], wst[b][:, :, :], ACT.Copy))
                w_split[i] = w_ready[n, e] = dve("f_wl", [hi], lambda g: g.tensor_tensor(
                    wlo[n][:, e, :, :], wst[b][:, :, :], whi[n][:, e, :, :].bitcast(fp32), ALU.subtract))

            NS = NCH * NX
            y_ready, gate_ready, acc_ready = {}, {}, {}
            l1, l2, l3, h1_ready, h2_ready, p1_free, p2_free, acc, stored = ({} for _ in range(9))
            pend = {}

            def load_x1(c):
                for d, sbuf in rows_of(x1_dram, c, x1[c % 2], False):
                    pend["x1", c] = dma("sync", f"f_ld{c % 2}", [stored.get(c - 2)], d, sbuf)

            def pre_norm(c):
                rs = row_stats("f", c, x1[c % 2], ST, MV, [pend["x1", c], pend.get(("y", c - 1))])
                pend["y", c] = normalize("f", c, y, x1[c % 2], MV, [rs, pend.get(("yt", c - 1))])

            def pre_turn(c):
                b, nn = c % 2, nodes(c)
                pend["yt", c] = t = pe("f_yt", [pend["y", c], pend.get(("pm", c - 1))],
                                       [tr(pm[:, k * CH + j * P:k * CH + j * P + r], y[0:r, j, k * P:(k + 1) * P],
                                           ident[0:r, 0:r]) for j, r in tiles(c) for k in range(KC)])
                v = pm[:, :].rearrange("p (k n) -> p k n", k=KC)[:, :, 0:nn]
                h = act("f_yh", [t, l1.get(c * NX - NX - 1)], lambda g: g.activation(yhi[b][:, :, 0:nn], v, ACT.Copy))
                y_ready[c] = dve("f_yl", [h], lambda g: g.tensor_tensor(
                    ylo[b][:, :, 0:nn], v, yhi[b][:, :, 0:nn].bitcast(fp32), ALU.subtract))

            def pre_gate(c):
                b = c % 2
                lgp = pm[:, 0:TPC * NX].rearrange("p (j e) -> p j e", e=NX)
                prods = [(yhi[b], wrh), (yhi[b], wrl), (ylo[b], wrh)]
                t = pe("f_lg", [y_ready[c], wr_ready],
                       [mm(lgp[0:r, j, :], u[:, k, j * P:j * P + r], w[:, k, :], i == 0 and k == 0, i == 2 and k == KC - 1)
                        for j, r in tiles(c) for i, (u, w) in enumerate(prods) for k in range(KC)])
                for j, k, r in groups(c):
                    t1 = dve("f_g", [t, pend.get(("ex", c - 1))], lambda g, j=j, k=k, r=r: g.tensor_tensor(
                        lg[0:r, j:j + k, :], lgp[0:r, j:j + k, :],
                        br_all[0:r, :].unsqueeze(1).broadcast_to([r, k, NX]), ALU.add))
                pend["lg", c] = t1
                for j, k, r in groups(c):
                    t2 = dve("f_g", [t1], lambda g, j=j, k=k, r=r: g.tensor_reduce(
                        mx[0:r, j:j + k], lg[0:r, j:j + k, :], AX.X, ALU.max))
                for j, k, r in groups(c):
                    t3 = dve("f_g", [t2], lambda g, j=j, k=k, r=r: g.tensor_tensor(
                        lg[0:r, j:j + k, :], lg[0:r, j:j + k, :],
                        mx[0:r, j:j + k].unsqueeze(2).broadcast_to([r, k, NX]), ALU.subtract))
                for j, k, r in groups(c):
                    t4 = act("f_ex", [t3, gate_ready.get(c - 1)], lambda g, j=j, k=k, r=r: g.activation(
                        ex[0:r, j:j + k, :], lg[0:r, j:j + k, :], ACT.Exp))
                pend["ex", c] = t4
                for j, k, r in groups(c):
                    t5 = dve("f_g", [t4], lambda g, j=j, k=k, r=r: g.tensor_reduce(
                        sm[0:r, j:j + k], ex[0:r, j:j + k, :], AX.X, ALU.add))
                for j, k, r in groups(c):
                    t6 = dve("f_g", [t5], lambda g, j=j, k=k, r=r: g.reciprocal(sm[0:r, j:j + k], sm[0:r, j:j + k]))
                for j, k, r in groups(c):
                    gate_ready[c] = dve("f_g", [t6], lambda g, j=j, k=k, r=r, b=b: g.tensor_tensor(
                        gate[b][0:r, j:j + k, :], ex[0:r, j:j + k, :],
                        sm[0:r, j:j + k].unsqueeze(2).broadcast_to([r, k, NX]), ALU.mult))

            def pre_bias_turn(c):
                b, nn = c % 2, nodes(c)
                t = pe("f_gt", [gate_ready[c]],
                       [tr(pm[0:NX, CH + j * P:CH + j * P + r], gate[b][0:r, j, :], ident[0:r, 0:r]) for j, r in tiles(c)])
                pend["gt", c] = act("f_ge", [t, pend.get(("bo", c - 1))], lambda g: g.activation(
                    gT[:, 0:nn], pm[0:NX, CH:CH + nn], ACT.Copy))

            def pre_bias(c):
                b = c % 2
                v = pm[:, :].rearrange("p (j n) -> p j n", n=C)
                pend["bo", c] = t = pe("f_bo", [pend["gt", c], pend["lg", c]],
                                       [mm(v[0:r, j, :], gT[:, j * P:j * P + r], bo_sb[:, :], True, True) for j, r in tiles(c)])
                for j, k, r in groups(c):
                    pend["pm", c] = acc_ready[c] = dve("f_ac", [t], lambda g, j=j, k=k, r=r: g.tensor_tensor(
                        x1[b][0:r, j:j + k, :], v[0:r, j:j + k, :], x1[b][0:r, j:j + k, :], ALU.add))

            def three(w, xh, xl, e, c, o):
                nn = nodes(c)
                pr = [(whi[w], xh), (whi[w], xl), (wlo[w], xh)]
                return [mm(o[:, m, 0:nn], ww[:, e, k, m * P:(m + 1) * P], xx[:, k, 0:nn], i == 0 and k == 0,
                           i == 2 and k == KC - 1)
                        for m in range(KC) for i, (ww, xx) in enumerate(pr) for k in range(KC)]

            def hidden(l, p, prod, i, c, e, reader):
                nn, b = nodes(c), i % 2
                for m in range(KC):
                    col = slice(e * KC + m, e * KC + m + 1)
                    hi = act(f"f_a{l}", [prod, reader, terms], lambda g, m=m, col=col: g.activation(
                        hhi[l][b][:, m, 0:nn], p[:, m, 0:nn], ACT.Relu, bias=shift[l][:, col], scale=scale[l][:, col]))
                for m in range(KC):
                    col = slice(e * KC + m, e * KC + m + 1)
                    full = act(f"f_a{l}", [pend.get(("lo", l))], lambda g, m=m, col=col: g.activation(
                        hf[l][:, m, 0:nn], p[:, m, 0:nn], ACT.Relu, bias=shift[l][:, col], scale=scale[l][:, col]))
                lo = dve(f"f_l{l}", [full], lambda g: g.tensor_tensor(
                    hlo[l][b][:, :, 0:nn], hf[l][:, :, 0:nn], hhi[l][b][:, :, 0:nn].bitcast(fp32), ALU.subtract))
                pend["lo", l] = lo
                return full, lo

            load_x1(0)
            pre_norm(0)
            pre_turn(0)
            pre_gate(0)
            pre_bias_turn(0)
            pre_bias(0)
            load_x1(1)
            for n in names:
                split_weight(n, 0)
            for i in range(NS + 2):
                c, e = divmod(i, NX)
                if i < NS:
                    if c == 0 and e + 1 < NX:
                        for n in names:
                            split_weight(n, e + 1)
                    l1[i] = pe("f_m1", [y_ready[c], w_ready["W1", e], p1_free.get(i - 1)],
                               three("W1", yhi[c % 2], ylo[c % 2], e, c, p1))
                    p1_free[i], h1_ready[i] = hidden(0, p1, l1[i], i, c, e, l2.get(i - 2))
                    if c + 1 < NCH:
                        if e == 2 and c + 1 > 1:
                            load_x1(c + 1)
                        if e == 3:
                            pre_norm(c + 1)
                        if e == 4:
                            pre_turn(c + 1)
                        if e == 5:
                            pre_gate(c + 1)
                        if e == 6:
                            pre_bias_turn(c + 1)
                        if e == 7:
                            pre_bias(c + 1)
                if 1 <= i <= NS:
                    q = i - 1
                    cq, eq = divmod(q, NX)
                    l2[q] = pe("f_m2", [h1_ready[q], w_ready["W2", eq], p2_free.get(q - 1)],
                               three("W2", hhi[0][q % 2], hlo[0][q % 2], eq, cq, p2))
                    p2_free[q], h2_ready[q] = hidden(1, p2, l2[q], q, cq, eq, l3.get(q - 2))
                if i >= 2:
                    q = i - 2
                    cq, eq = divmod(q, NX)
                    b = q % 2
                    pr = [(hhi[1][b], whi["Wo"]), (hhi[1][b], wlo["Wo"]), (hlo[1][b], whi["Wo"])]
                    l3[q] = pe("f_m3", [h2_ready[q], w_ready["Wo", eq], acc.get(q - 1)],
                               [mm(p3[0:r, j, :], xx[:, k, j * P:j * P + r], ww[:, eq, k, :], n == 0 and k == 0,
                                   n == 2 and k == KC - 1)
                                for j, r in tiles(cq) for n, (xx, ww) in enumerate(pr) for k in range(KC)])
                    for j, r in tiles(cq):
                        acc[q] = dve("f_c3", [l3[q], acc_ready[cq] if eq == 0 else acc[q - 1]],
                                     lambda g, j=j, r=r, cq=cq, eq=eq: g.scalar_tensor_tensor(
                                         x1[cq % 2][0:r, j, :], p3[0:r, j, :], gate[cq % 2][0:r, j, eq:eq + 1],
                                         x1[cq % 2][0:r, j, :], ALU.mult, ALU.add))
                    if eq == NX - 1:
                        for d, sbuf in rows_of(out, cq, x1[cq % 2], True):
                            stored[cq] = dma("sync", f"f_st{cq % 2}", [acc[q]], d, sbuf)
            step("sync", stream("fence"), [stored[NCH - 1], stored[NCH - 2]], lambda g: g.nop())
            run_block()


def kernel(**inputs):
    import numpy as np
    import concourse.bacc as bacc
    from concourse import mybir
    from concourse.bass_utils import run_bass_kernel_spmd

    nc = bacc.Bacc("TRN2", target_bir_lowering=False, num_devices=1)
    arrays, aps = {}, {}
    for name, value in inputs.items():
        v = np.ascontiguousarray(value)
        arrays[f"in_{name}"] = v
        aps[name] = nc.dram_tensor(f"in_{name}", v.shape, mybir.dt.from_np(v.dtype), kind="ExternalInput").ap()
    out = nc.dram_tensor("out_x", arrays["in_x"].shape, mybir.dt.float32, kind="ExternalOutput").ap()
    build(nc, aps, out)
    r = run_bass_kernel_spmd(nc, [arrays], core_ids=[0])
    return r.results[0]["out_x"]
```

```python
def build(nc, a, out):
    import concourse.bass as bass
    from concourse import mybir
    from contextlib import ExitStack

    fp32, f32r, i32 = mybir.dt.float32, mybir.dt.float32r, mybir.dt.int32
    ALU, ACT, AX = mybir.AluOpType, mybir.ActivationFunctionType, mybir.AxisListType

    P = 128
    N, C = a["x"].shape
    E = a["src"].shape[0]
    NX = a["L0_ffn_Wr"].shape[1]
    KC = C // P
    TPC = 4
    CH = TPC * P
    NCH = -(-N // CH)
    ET = -(-E // P)
    EB = -(-ET // P)
    LN_EPS, BN_EPS, FFN_EPS = 1e-5, 1e-5, 1e-3
    assert C == KC * P and N > P and E > P

    def nodes(c):
        return min(CH, N - c * CH)

    def tiles(c):
        return [(j, min(P, nodes(c) - j * P)) for j in range(-(-nodes(c) // P))]

    def groups(c):
        full, rest = divmod(nodes(c), P)
        return ([(0, full, P)] if full else []) + ([(full, 1, rest)] if rest else [])

    top = ExitStack()

    class Stream:

        def __init__(self, name, by=1):
            self.sem, self.n, self.by = top.enter_context(nc.semaphore(name)), 0, by

    streams = {}

    def stream(name, by=1):
        if name not in streams:
            streams[name] = Stream(name, by)
        return streams[name]

    queues = {e: [] for e in ("sync", "scalar", "vector", "gpsimd", "tensor")}
    waited = {}

    def step(engine, signal, waits, fn):
        need = {}
        for w in waits:
            if w is not None:
                need[w[0]] = max(need.get(w[0], 0), w[1])
        todo = [(s, v) for s, v in need.items() if waited.get((engine, s), 0) < v]
        for s, v in todo:
            waited[(engine, s)] = v
        token = None
        if signal is not None:
            signal.n += signal.by
            token = (signal, signal.n)

        def emit(eng):
            for s, v in todo:
                eng.wait_ge(s.sem, v)
            ins = fn(eng)
            if signal is not None:
                ins.then_inc(signal.sem, signal.by)
        queues[engine].append(emit)
        return token

    entry = {
        "sync": lambda b: b.sync, "scalar": lambda b: b.scalar, "vector": lambda b: b.vector,
        "gpsimd": lambda b: b.gpsimd, "tensor": lambda b: b.tensor,
    }

    def run_block():
        with nc.Block() as block:
            for name in queues:
                def body(eng, todo=list(queues[name])):
                    for emit in todo:
                        emit(eng)
                entry[name](block)(body)
                queues[name].clear()

    def dma(engine, name, waits, dst, src):
        return step(engine, stream(name, 16), waits, lambda g: g.dma_start(dst, src))

    def dve(name, waits, fn):
        return step("vector", stream(name), waits, fn)

    def act(name, waits, fn):
        return step("scalar", stream(name), waits, fn)

    def pool(name, waits, fn):
        return step("gpsimd", stream(name), waits, fn)

    def pe(name, waits, fns):
        def emit(g):
            for f in fns:
                ins = f(g)
            return ins
        return step("tensor", stream(name), waits, emit)

    def mm(o, l, r, start, stop):
        return lambda g: nc.tensor.matmul(o, l, r, start=start, stop=stop)

    def tr(o, i, ident_rows):
        return lambda g: nc.tensor.transpose(o, i, ident_rows)

    def rows_of(dram, c, buf, write):
        for j, k, r in groups(c):
            lo = c * CH + j * P
            d = dram[lo:lo + k * r, :].rearrange("(k p) n -> p k n", p=r)
            s = buf[0:r, j:j + k, :]
            yield (d, s) if write else (s, d)

    with top:
        def sb(ctx, name, shape, dt=fp32):
            return ctx.enter_context(nc.sbuf_tensor(name, shape, dt))

        def ps(ctx, name, shape):
            return ctx.enter_context(nc.psum_tensor(name, shape, fp32))

        h_dram = [nc.dram_tensor(f"h{i}", (N, C), fp32, kind="Internal").ap() for i in range(2)]
        u_dram = nc.dram_tensor("u", (NCH, P, KC * CH), fp32, kind="Internal").ap()
        base_dram = nc.dram_tensor("tile_base", (EB, P), i32, kind="Internal").ap()

        ident = sb(top, "ident", [P, P])
        eps_ln = sb(top, "eps_ln", [P, 1])
        eps_ffn = sb(top, "eps_ffn", [P, 1])
        ones_row = sb(top, "ones_row", [1, P])
        ln1 = sb(top, "ln1", [P, NCH * TPC, 3])
        conv_p = sb(top, "conv_p", [P, 10 * KC])
        ffn_p = [sb(top, f"ffn_p{i}", [P, 5 * NX * KC]) for i in range(2)]
        wr_raw = sb(top, "wr_raw", [P, KC, P])
        br_col = sb(top, "br_col", [NX, 1])
        bo_sb = sb(top, "bo_sb", [NX, C])

        conv_names = [f"L0_gnn_{n}" for c in "12" for n in (f"c{c}_b2", f"c{c}_g", f"c{c}_b", f"bn{c}_g", f"bn{c}_b")]

        def conv_col(layer, which, m):
            i = KC * (5 * layer + which) + m
            return conv_p[:, i:i + 1]

        def conv_cols(layer, which):
            i = KC * (5 * layer + which)
            return conv_p[:, i:i + KC]

        sc2, sh2 = sb(top, "sc2", [P, KC]), sb(top, "sh2", [P, KC])
        WB = 4
        wst = [sb(top, f"wst{i}", [P, KC, C]) for i in range(WB)]

        names = ("W1", "W2", "Wo")
        w_order = [(n, e) for e in range(NX) for n in names]

        def load_ffn_weight(i, waits):
            n, e = w_order[i]
            return dma("sync", f"f_wld{i % WB}", waits, wst[i % WB][:, :, :],
                       a[f"L0_ffn_{n}"][e].rearrange("(k p) n -> p k n", p=P))

        convs = ExitStack()
        w1 = [sb(convs, f"w1_{i}", [P, KC, C]) for i in range(2)]
        w2 = [sb(convs, f"w2_{i}", [P, KC, C]) for i in range(2)]
        b1_all = [sb(convs, f"b1_{i}", [P, C]) for i in range(2)]
        AW = N + P
        agg = sb(convs, "agg", [P, KC, AW])
        edges = ExitStack()
        src_col = sb(edges, "src_col", [P, EB * P], i32)
        rel_col = sb(edges, "rel_col", [P, EB * P])
        ew_col = sb(edges, "ew_col", [P, EB * P])
        base_row = sb(edges, "base_row", [1, EB * P], i32)
        lane = sb(edges, "lane", [P, P])
        far = sb(edges, "far", [1, 1], i32)

        aggregated = {}

        def row_stats(tag, c, x, stats, mv, waits):
            for j, r in tiles(c):
                t = dve(f"{tag}_st", waits, lambda g, j=j, r=r: g.bn_stats(stats[0:r, j, :], x[0:r, j, :]))
            for j, r in tiles(c):
                t2 = dve(f"{tag}_ag", [t], lambda g, j=j, r=r: g.bn_aggr(mv[0:r, j, 0:2], stats[0:r, j, :]))
            aggregated[tag, c] = t2
            for j, k, r in groups(c):
                t3 = act(f"{tag}_sd", [t2], lambda g, j=j, k=k, r=r: g.activation(
                    mv[0:r, j:j + k, 1], mv[0:r, j:j + k, 1], ACT.Sqrt, bias=eps_ln[0:r, :]))
            return t3

        def row_rstd(tag, c, mv, waits):
            for j, k, r in groups(c):
                t = dve(f"{tag}_rs", waits, lambda g, j=j, k=k, r=r: g.reciprocal(
                    mv[0:r, j:j + k, 1], mv[0:r, j:j + k, 1]))
            return t

        def row_minus_mean(tag, c, mv, waits):
            for j, k, r in groups(c):
                t = dve(f"{tag}_mm", waits, lambda g, j=j, k=k, r=r: g.tensor_scalar(
                    mv[0:r, j:j + k, 2], mv[0:r, j:j + k, 0], -1.0, None, ALU.mult))
            return t

        def center(tag, c, dst, x, mv, waits, on_vector):
            last = {}
            for j, r in tiles(c):
                if j >= TPC - on_vector:
                    last["v"] = dve(f"{tag}_cv", waits, lambda g, j=j, r=r: g.tensor_scalar(
                        dst[0:r, j, :], x[0:r, j, :], mv[0:r, j, 0:1], None, ALU.subtract))
                else:
                    last["a"] = act(f"{tag}_ca", waits, lambda g, j=j, r=r: g.activation(
                        dst[0:r, j, :], x[0:r, j, :], ACT.Identity, bias=mv[0:r, j, 2:3]))
            return list(last.values())

        def normalize(tag, c, dst, x, mv, waits):
            for j, r in tiles(c):
                t = step("vector", stream(f"{tag}_nm"), waits, lambda g, j=j, r=r: g.tensor_scalar(
                    dst[0:r, j, :], x[0:r, j, :], mv[0:r, j, 0:1], mv[0:r, j, 1:2], ALU.subtract, ALU.mult))
            return t

        def passes(x, w):
            return [(x[0], w[0]), (x[0], w[1]), (x[1], w[0])]

        def split_conv_weight(s, name, w):
            hi, lo = sb(s, f"{name}_hi", [P, KC, C], f32r), sb(s, f"{name}_lo", [P, KC, C], f32r)
            t = act("w_hi", [], lambda g: g.activation(hi[:, :, :], w[:, :, :], ACT.Copy))
            return (hi, lo), dve("w_lo", [t], lambda g: g.tensor_tensor(
                lo[:, :, :], w[:, :, :], hi[:, :, :].bitcast(fp32), ALU.subtract))

        def hidden_product(tag, c, pairs, pH, waits):
            return pe(f"{tag}_h", waits,
                      [mm(pH[0:r, j, :], x[:, k, j * P:j * P + r], w[:, k, :], n == 0 and k == 0,
                          n == len(pairs) - 1 and k == KC - 1)
                       for j, r in tiles(c) for n, (x, w) in enumerate(pairs) for k in range(KC)])

        def hidden_out(tag, c, bias, hbuf, pH, h_out, waits, rstd=None):
            for j, r in tiles(c) if rstd is not None else []:
                biased = dve(f"{tag}_hb", waits, lambda g, j=j, r=r: g.scalar_tensor_tensor(
                    hbuf[0:r, j, :], pH[0:r, j, :], rstd[0:r, j, :], bias[0:r, :], ALU.mult, ALU.add))
            for j, k, r in groups(c) if rstd is None else []:
                biased = dve(f"{tag}_hb", waits, lambda g, j=j, k=k, r=r: g.tensor_tensor(
                    hbuf[0:r, j:j + k, :], pH[0:r, j:j + k, :],
                    bias[0:r, :].unsqueeze(1).broadcast_to([r, k, C]), ALU.add))
            for j, k, r in groups(c):
                v = hbuf[0:r, j:j + k, :]
                relu = act(f"{tag}_hr", [biased], lambda g, v=v: g.activation(v, v, ACT.Relu))
            for d, sbuf in rows_of(h_out, c, hbuf, True):
                st = dma("sync", f"{tag}_hst{c % 3}", [relu], d, sbuf)
            return biased, st

        def last_stores(stored):
            step("sync", stream("fence"), [stored[c] for c in range(max(0, NCH - 3), NCH)], lambda g: g.nop())

        with ExitStack() as s:
            def in_agg(i, dt=fp32):
                v = agg[:, 0, i * EB * P:(i + 1) * EB * P]
                return (v if dt == fp32 else v.bitcast(dt)).rearrange("p (b e) -> p b e", e=P)
            assert 5 * EB * P <= AW
            raw = {"src": in_agg(0, i32), "dst": in_agg(1, i32), "ew": in_agg(2)}
            src_f, dst_f = in_agg(3), in_agg(4)
            tile_min = sb(s, "tile_min", [P, EB])
            tile_max = sb(s, "tile_max", [P, EB])
            span = sb(s, "span", [P, 1])
            base_i = sb(s, "base_i", [EB, P], i32)
            prow = [sb(s, f"prow{i}", [P, P]) for i in range(3)]
            brow = sb(s, "brow", [1, 2 * C])
            X = [sb(s, f"a_x{i}", [P, TPC, C]) for i in range(3)]
            Y = [sb(s, f"a_y{i}", [P, TPC, C]) for i in range(2)]
            YT = [sb(s, f"a_yt{i}", [P, KC, CH]) for i in range(2)]
            H = [sb(s, f"a_h{i}", [P, TPC, C]) for i in range(3)]
            ST = [sb(s, f"a_st{i}", [P, TPC, 6]) for i in range(2)]
            pT = [ps(s, f"a_pt{i}", [P, KC * CH]) for i in range(2)]
            pH = [ps(s, f"a_ph{i}", [P, TPC, C]) for i in range(2)]
            pT_free, pH_free = [[], []], [[], []]

            zi = pool("init", [], lambda g: g.memset(ident[:, :], 0.0))
            ident_ready = pool("init", [zi], lambda g: g.affine_select(
                out=ident[:, :], in_=ident[:, :], compare_op=ALU.not_equal, fill=1.0, base=0,
                pattern=[[-1, P]], channel_multiplier=1))
            pool("init", [], lambda g: g.memset(eps_ln[:, :], LN_EPS))
            eps_ready = pool("init", [], lambda g: g.memset(eps_ffn[:, :], FFN_EPS))
            wr_clear = pool("init", [], lambda g: g.memset(wr_raw[:, :, :], 0.0))
            ones_ready = pool("init", [], lambda g: g.memset(ones_row[:, :], 1.0))
            pool("init", [], lambda g: g.iota(lane[:, :], pattern=[[1, P]], base=0, channel_multiplier=0,
                                              allow_small_or_imprecise_dtypes=True))

            def load_x(c):
                for d, sbuf in rows_of(a["x"], c, X[c % 3], False):
                    ld = dma("sync", f"a_ld{c % 3}", normed.get(c - 3, []), d, sbuf)
                return ld

            normed, turned, evac, prod, hst, x_in, sd, minus, rstd = ({} for _ in range(9))
            for c in range(2):
                x_in[c] = load_x(c)

            for i, (n, l) in enumerate((("w1", 0), ("w1", 1), ("w2", 0), ("w2", 1))):
                w = (w1 if n == "w1" else w2)[l]
                t = dma("scalar", f"ld_w{i > 0}", [], w[:, :, :],
                        a[f"L0_gnn_c{l + 1}_{n}"].rearrange("(k p) n -> p k n", p=P))
                if i == 0:
                    w1_loaded = t
                    for layer in range(2):
                        dma("scalar", "ld_bias", [], brow[0:1, layer * C:(layer + 1) * C],
                            a[f"L0_gnn_c{layer + 1}_b1"].rearrange("(p n) -> p n", p=1))
                    bias_loaded = dma("scalar", "ld_bias", [], br_col[:, :],
                                      a["L0_ffn_br"].rearrange("(p n) -> p n", n=1))
            weights_loaded = t

            for r in raw.values():
                cleared = dve("clear", [], lambda g, r=r: g.memset(r[:, EB - 1, :], 0))
            loaded = {}
            full_blocks, last_tiles, last_edges = ET // P, (E - (ET // P) * P * P) // P, E % P
            for n, dram in (("src", a["src"]), ("dst", a["dst"]), ("ew", a["edge_weight"])):
                lo = full_blocks * P * P
                t = dma("gpsimd", f"ld_{n}", [], raw[n][:, 0:full_blocks, :],
                        dram[0:lo].rearrange("(b p e) -> p b e", p=P, e=P))
                if last_tiles:
                    t = dma("gpsimd", f"ld_{n}", [cleared], raw[n][0:last_tiles, EB - 1, :],
                            dram[lo:lo + last_tiles * P].rearrange("(p e) -> p e", e=P))
                if last_edges:
                    lo += last_tiles * P
                    t = dma("gpsimd", f"ld_{n}", [cleared],
                            raw[n][last_tiles:last_tiles + 1, EB - 1, 0:last_edges],
                            dram[lo:E].rearrange("(p e) -> p e", p=1))
                    if n == "dst":
                        need = P - last_edges
                        t = dma("gpsimd", f"ld_{n}", [],
                                raw[n][last_tiles:last_tiles + 1, EB - 1, last_edges:P],
                                dram[E - need:E].rearrange("(p e) -> p e", p=1))
                loaded[n] = t

            dma("gpsimd", "ld_par", [], bo_sb[:, :], a["L0_ffn_bo"])
            dma("gpsimd", "ld_par", [wr_clear], wr_raw[:, :, 0:NX], a["L0_ffn_Wr"].rearrange("(k p) n -> p k n", p=P))
            for i, n in enumerate(conv_names):
                dma("gpsimd", "ld_par", [], prow[2][KC * i:KC * (i + 1), :], a[n].rearrange("(m p) -> m p", p=P))
            for layer in range(2):
                for i, n in enumerate(("g", "b", "be", "m", "v")):
                    w = NX * KC
                    params = dma("gpsimd", "ld_par", [], prow[layer][w * i:w * (i + 1), :],
                                 a[f"L0_ffn_{n}{layer + 1}"].rearrange("e (m p) -> (e m) p", p=P))

            done = {}

            def side_params(b):
                cols = [0, P, 2 * P]
                turned_p = pe("p_par", [params, ident_ready] + pT_free[b],
                              [tr(pT[b][:, i * P:i * P + w], prow[i][0:w, :], ident[0:w, 0:w])
                               for i, w in enumerate((5 * NX * KC, 5 * NX * KC, 10 * KC))])
                for i, (dst, w) in enumerate(((ffn_p[0], 5 * NX * KC), (ffn_p[1], 5 * NX * KC), (conv_p, 10 * KC))):
                    t = dve("v_par", [turned_p], lambda g, dst=dst, i=i, w=w: g.tensor_copy(
                        dst[:, :], pT[b][:, i * P:i * P + w]))
                pT_free[b] = [t]

            def side_index(b):
                done["src"] = dve("v_idx", [loaded["src"], cleared], lambda g: g.tensor_copy(src_f[:, :, :], raw["src"][:, :, :]))
                c_dst = dve("v_idx", [loaded["dst"]], lambda g: g.tensor_copy(dst_f[:, :, :], raw["dst"][:, :, :]))
                done["min"] = dve("v_idx", [c_dst], lambda g: g.tensor_reduce(tile_min[:, :], dst_f[:, :, :], AX.X, ALU.min))
                done["max"] = dve("v_idx", [c_dst], lambda g: g.tensor_reduce(tile_max[:, :], dst_f[:, :, :], AX.X, ALU.max))

            def side_rel(b):
                for e in range(EB):
                    done["dst"] = dve("v_idx", [done["min"]], lambda g, e=e: g.tensor_scalar(
                        dst_f[:, e, :], dst_f[:, e, :], tile_min[:, e:e + 1], None, ALU.subtract))
                m = dve("v_idx", [done["max"]], lambda g: g.tensor_tensor(tile_max[:, :], tile_max[:, :], tile_min[:, :], ALU.subtract))
                done["span"] = dve("v_idx", [m], lambda g: g.tensor_reduce(span[:, :], tile_max[:, :], AX.X, ALU.max))

            def side_base(b):
                m = pe("p_idx", [done["span"], ident_ready] + pT_free[b],
                       [tr(pT[b][0:1, 0:P], span[:, :], ident[:, :]),
                        tr(pT[b][0:EB, P:2 * P], tile_min[:, :], ident[:, :])])
                base_ready = dve("v_idx", [m], lambda g: g.tensor_copy(base_i[:, :], pT[b][0:EB, P:2 * P]))
                m = dve("v_idx", [m], lambda g: g.tensor_reduce(span[0:1, :], pT[b][0:1, 0:P], AX.X, ALU.max))
                pT_free[b] = [m]
                m = dve("v_idx", [m], lambda g: g.tensor_copy(far[:, :], span[0:1, :]))
                m = dve("v_idx", [m], lambda g: g.tensor_single_scalar(
                    far[:, :], far[:, :], P.bit_length() - 1, ALU.arith_shift_right))
                stored = dma("scalar", "st_base", [base_ready], base_dram, base_i[:, :])
                done["base"] = dma("scalar", "ld_base", [stored], base_row[:, :],
                                   base_dram.rearrange("(o b) p -> o (b p)", o=1))

            def side_turn(srcbuf, dstbuf, key, lo, k):
                def go(b):
                    ready = done[key] if key in done else loaded[key]
                    t = pe("p_idx", [ready, cleared, ident_ready] + pT_free[b],
                           [tr(pT[b][:, i * P:(i + 1) * P], srcbuf[:, lo + i, :], ident[:, :]) for i in range(k)])
                    t = dve("v_turn", [t], lambda g: g.tensor_copy(dstbuf[:, lo * P:(lo + k) * P], pT[b][:, 0:k * P]))
                    pT_free[b] = [t]
                    done["turn"] = t
                return go

            def side_clear(b):
                for k in range(KC):
                    pool("clear_agg", [done["turn"]], lambda g, k=k: g.memset(agg[:, k, :], 0.0))

            side = [side_index, side_rel, side_base]
            per = (KC * CH) // P
            for lo in range(0, EB, per):
                for srcbuf, dstbuf, key in ((src_f, src_col, "src"), (raw["ew"], ew_col, "ew"), (dst_f, rel_col, "dst")):
                    side.append(side_turn(srcbuf, dstbuf, key, lo, min(per, EB - lo)))
            side += [side_clear, side_params]

            def spread_biases():
                flat = pH[1][:, :, :].rearrange("p j n -> p (j n)")
                t = pe("p_par", [ones_ready, bias_loaded],
                       [mm(flat[:, l * C:(l + 1) * C], ones_row[:, :], brow[0:1, l * C:(l + 1) * C], True, True)
                        for l in range(2)])
                for l in range(2):
                    t1 = dve("v_bias", [t], lambda g, l=l: g.tensor_copy(b1_all[l][:, :], flat[:, l * C:(l + 1) * C]))
                pH_free[1] = [t1]
                return t1

            def mv_of(c):
                return ln1[:, c * TPC:(c + 1) * TPC, :]

            for i in range(NCH + 4):
                q = i - 2
                if 0 <= q < NCH:
                    b, nn = q % 2, nodes(q)
                    turned[q] = pe("a_t", normed[q] + [ident_ready] + pT_free[b],
                                   [tr(pT[b][:, k * CH + j * P:k * CH + j * P + r], Y[b][0:r, j, k * P:(k + 1) * P],
                                       ident[0:r, 0:r]) for j, r in tiles(q) for k in range(KC)])
                    evac[q] = act("a_ev", [turned[q], prod.get(q - 2)], lambda g, b=b, nn=nn: g.activation(
                        YT[b][:, :, 0:nn], pT[b][:, :].rearrange("p (k n) -> p k n", k=KC)[:, :, 0:nn], ACT.Copy))
                    pT_free[b] = [evac[q]]
                q = i - 3
                if 0 <= q < NCH:
                    prod[q] = hidden_product("a", q, [(YT[q % 2], w1[0])], pH[q % 2],
                                             [evac[q], w1_loaded] + pH_free[q % 2])
                q = i - 1
                if 0 <= q < NCH:
                    normed[q] = center("a", q, Y[q % 2], X[q % 3], mv_of(q), [minus[q], turned.get(q - 2)], 1)
                    rstd[q] = row_rstd("a", q, mv_of(q), [sd[q]])
                q = i - 4
                if 0 <= q < NCH:
                    biased, hst[q] = hidden_out("a", q, b1_all[0], H[q % 3], pH[q % 2], h_dram[0],
                                                [prod[q], bias_ready, rstd[q], hst.get(q - 3)], mv_of(q)[:, :, 1:2])
                    pH_free[q % 2] = [biased]
                q = i
                if q < NCH:
                    sd[q] = row_stats("a", q, X[q % 3], ST[q % 2], mv_of(q), [x_in[q], eps_ready])
                    minus[q] = row_minus_mean("a", q, mv_of(q), [aggregated["a", q]])
                    if q + 2 < NCH:
                        x_in[q + 2] = load_x(q + 2)
                if i == 1:
                    bias_ready = spread_biases()
                if i >= 5 and side:
                    side.pop(0)((i - 2) % 2 if i - 2 >= NCH else (i - 1) % 2)
            assert not side
            last_stores(hst)
            dve("seen", [done["base"], weights_loaded, params], lambda g: g.memset(base_i[0:1, 0:1], 0))
            run_block()

        def aggregate(layer):
            R, RO, RP = 10, 4, 4
            with ExitStack() as s:
                G = [sb(s, f"g{layer}_{i}", [P, C]) for i in range(R)]
                OH = [sb(s, f"oh{layer}_{i}", [P, P]) for i in range(RO)]
                pA = [ps(s, f"pa{layer}_{i}", [P, 512]) for i in range(RP)]
                sums, onehot, added = {}, {}, {}
                t = f"g{layer}"
                LAG = 2
                regs = {}
                BATCH = 16

                def load_bases(g, e):
                    if not regs:
                        regs["r"] = [g.alloc_register(f"{t}_base{i}") for i in range(BATCH)]
                    k = min(BATCH, ET - e)
                    return g.load(regs["r"][0:k], base_row[0:1, e:e + k])

                for e in range(ET + LAG):
                    if e < ET:
                        gathered = step("gpsimd", stream(f"g_ga{e % R}", 16), [sums.get(e - R)],
                                        lambda g, e=e: g.indirect_dma_start(
                                            G[e % R][:, :], None, h_dram[layer],
                                            bass.IndirectOffsetOnAxis(ap=src_col[:, e:e + 1], axis=0)))
                        onehot[e] = dve("g_oh", [sums.get(e - RO)], lambda g, e=e: g.tensor_scalar(
                            OH[e % RO][:, :], lane[:, :], rel_col[:, e:e + 1], ew_col[:, e:e + 1],
                            ALU.is_equal, ALU.mult))
                        sums[e] = pe("g_mm", [gathered, onehot[e], added.get(e - RP)],
                                     [mm(pA[e % RP][:, k * P:(k + 1) * P], G[e % R][:, k * P:(k + 1) * P],
                                         OH[e % RO][:, :], True, True) for k in range(KC)])
                    if e >= LAG:
                        q = e - LAG

                        def add(g, q=q):
                            if q % BATCH == 0:
                                load_bases(g, q)
                            base = g.snap(regs["r"][q % BATCH], min_val=0, max_val=N - 1)
                            win = agg[:, :, bass.ds(base, P)]
                            return g.tensor_tensor(win, win, pA[q % RP][:, 0:KC * P].rearrange(
                                "p (k n) -> p k n", k=KC), ALU.add)
                        added[q] = dve("g_add", [sums[q], added.get(q - 1)], add)
                far_windows(layer, s, G[0], OH[0], pA[0])
                run_block()

        far_sem = {n: top.enter_context(nc.semaphore(f"far_{n}"))
                   for n in ("idx", "gathered", "landed", "onehot", "sums", "added", "fixed", "turn")}

        def far_windows(layer, s, G, OH, pA):
            t = f"x{layer}"
            idx = sb(s, f"{t}_idx", [P, 1], i32)
            rel_w = sb(s, f"{t}_rel", [P, EB * P])
            rel_e, ew_e = sb(s, f"{t}_rel_e", [P, 1]), sb(s, f"{t}_ew_e", [P, 1])
            base_f = sb(s, f"{t}_base_f", [1, EB * P])
            base_w = sb(s, f"{t}_base_w", [1, EB * P], i32)
            sem = far_sem

            def take(g, name):
                g.wait_ge(sem[name], 1)
                g.sem_clear(sem[name])

            def loops(g):
                count = g.alloc_register(f"{t}_far")
                g.load(count, far[0:1, 0:1])
                return count

            def pool_loop(g):
                count = loops(g)
                with g.If_ne(count, 0):
                    with g.Fori(0, count):
                        with g.Fori(0, ET) as e:
                            g.tensor_copy(idx[:, :], src_col[:, bass.ds(e, 1)]).then_inc(sem["idx"], 1)
                            take(g, "idx")
                            g.indirect_dma_start(G[:, :], None, h_dram[layer], bass.IndirectOffsetOnAxis(
                                ap=idx[:, :], axis=0)).then_inc(sem["gathered"], 16)
                            g.wait_ge(sem["gathered"], 16)
                            g.dma_reset(range(sem["gathered"].num, sem["gathered"].num + 1))
                            g.sem_clear(sem["gathered"])
                            g.sem_inc(sem["landed"], 1)
                            take(g, "added")
                return g.nop()

            def pe_loop(g):
                count = loops(g)
                with g.If_ne(count, 0):
                    with g.Fori(0, count):
                        with g.Fori(0, ET):
                            take(g, "landed")
                            take(g, "onehot")
                            for k in range(KC):
                                ins = nc.tensor.matmul(pA[:, k * P:(k + 1) * P], G[:, k * P:(k + 1) * P], OH[:, :],
                                                       start=True, stop=True)
                            ins.then_inc(sem["sums"], 1)
                return g.nop()

            def dve_loop(g):
                def done(ins):
                    ins.then_inc(sem["fixed"], 1)
                    take(g, "fixed")

                count = loops(g)
                with g.If_ne(count, 0):
                    done(g.tensor_copy(rel_w[:, :], rel_col[:, :]))
                    done(g.tensor_copy(base_f[:, :], base_row[:, :]))
                    with g.Fori(0, count):
                        done(g.tensor_scalar(rel_w[:, :], rel_w[:, :], float(P), None, ALU.subtract))
                        done(g.tensor_scalar(base_f[:, :], base_f[:, :], float(P), float(N), ALU.add, ALU.min))
                        done(g.tensor_copy(base_w[:, :], base_f[:, :]))
                        with g.Fori(0, ET) as e:
                            done(g.tensor_copy(rel_e[:, :], rel_w[:, bass.ds(e, 1)]))
                            done(g.tensor_copy(ew_e[:, :], ew_col[:, bass.ds(e, 1)]))
                            g.tensor_scalar(OH[:, :], lane[:, :], rel_e[:, :], ew_e[:, :], ALU.is_equal,
                                            ALU.mult).then_inc(sem["onehot"], 1)
                            base = g.value_load(base_w[0:1, bass.ds(e, 1)], min_val=0, max_val=N)
                            take(g, "sums")
                            win = agg[:, :, bass.ds(base, P)]
                            g.tensor_tensor(win, win, pA[:, 0:KC * P].rearrange("p (k n) -> p k n", k=KC),
                                            ALU.add).then_inc(sem["turn"], 1)
                            take(g, "turn")
                            g.sem_inc(sem["added"], 1)
                return g.nop()

            last_add, last_sum = stream("g_add"), stream("g_mm")
            done_add, done_sum = (last_add, last_add.n), (last_sum, last_sum.n)
            step("gpsimd", None, [done_sum], pool_loop)
            step("vector", None, [done_add, done_sum], dve_loop)
            step("tensor", None, [done_add], pe_loop)

        def norm_terms(tag, layer, which, stats, scale, shift, waits):
            mv = tag_mv[tag]
            for m in range(KC):
                t = dve("bn_ag", waits, lambda g, m=m: g.bn_aggr(
                    mv[:, m, :], stats[:, m, :, :].rearrange("p c s -> p (c s)")))
            t = act("bn_sd", [t], lambda g: g.activation(mv[:, :, 1], mv[:, :, 1], ACT.Sqrt, bias=eps_ln[:, :]))
            t = dve("bn_tm", [t], lambda g: g.reciprocal(mv[:, :, 1], mv[:, :, 1]))
            t = dve("bn_tm", [t], lambda g: g.tensor_tensor(scale[:, :], mv[:, :, 1], conv_cols(layer, which), ALU.mult))
            t = dve("bn_tm", [t], lambda g: g.tensor_tensor(mv[:, :, 0], mv[:, :, 0], scale[:, :], ALU.mult))
            return dve("bn_tm", [t], lambda g: g.tensor_tensor(shift[:, :], conv_cols(layer, which + 1), mv[:, :, 0], ALU.subtract))

        tag_mv, w_in = {}, {}

        def chunk_cols(c):
            return u_dram[c, :, :].rearrange("p (k n) -> p k n", k=KC)[:, :, 0:nodes(c)]

        def conv_tail(layer, s, store_u=False):
            t = f"c{layer}"
            pZ = [ps(s, f"{t}_pz{i}", [P, KC, CH]) for i in range(2)]
            stats = [sb(s, f"{t}_st{i}", [P, KC, NCH, 6]) for i in range(2)]
            for i in range(2):
                tag_mv[f"{t}{i}"] = sb(s, f"{t}_mv{i}", [P, KC, 2])
            sc1, sh1 = sb(s, f"{t}_sc1", [P, KC]), sb(s, f"{t}_sh1", [P, KC])
            w2s, w2_split = split_conv_weight(s, f"{t}_w2", w2[layer])
            halves = ExitStack()
            AH = [sb(halves, f"{t}_ah{i}", [P, KC, CH], f32r) for i in range(3)]
            AL = [sb(halves, f"{t}_al{i}", [P, KC, CH], f32r) for i in range(3)]
            hi, cut, prod, ev, st = {}, {}, {}, {}, None
            for i in range(NCH + 4):
                c = i
                if c < NCH:
                    nn, lo, b = nodes(c), c * CH, c % 3
                    hi[c] = act("c_ah", [prod.get(c - 3)], lambda g, nn=nn, lo=lo, b=b: g.activation(
                        AH[b][:, :, 0:nn], agg[:, :, lo:lo + nn], ACT.Copy))
                c = i - 1
                if 0 <= c < NCH:
                    nn, lo, b = nodes(c), c * CH, c % 3
                    cut[c] = dve("c_al", [hi[c], prod.get(c - 3)], lambda g, nn=nn, lo=lo, b=b: g.tensor_tensor(
                        AL[b][:, :, 0:nn], agg[:, :, lo:lo + nn], AH[b][:, :, 0:nn].bitcast(fp32), ALU.subtract))
                c = i - 2
                if 0 <= c < NCH:
                    nn = nodes(c)
                    prod[c] = pe("c_z", [cut[c], w2_split, ev.get(c - 2)],
                                 [mm(pZ[c % 2][:, m, 0:nn], w[:, k, m * P:(m + 1) * P], x[:, k, 0:nn],
                                     n == 0 and k == 0, n == 2 and k == KC - 1)
                                  for m in range(KC) for n, (x, w) in enumerate(passes((AH[c % 3], AL[c % 3]), w2s))
                                  for k in range(KC)])
                c = i - 3
                if 0 <= c < NCH:
                    nn, lo = nodes(c), c * CH
                    for m in range(KC):
                        ev[c] = act("c_ze", [prod[c]], lambda g, m=m, nn=nn, lo=lo, c=c: g.activation(
                            agg[:, m, lo:lo + nn], pZ[c % 2][:, m, 0:nn], ACT.Identity, bias=conv_col(layer, 0, m)))
                c = i - 4
                if 0 <= c < NCH:
                    nn, lo = nodes(c), c * CH
                    for m in range(KC):
                        st = dve("c_zs", [ev[c]], lambda g, m=m, nn=nn, lo=lo, c=c: g.bn_stats(
                            stats[0][:, m, c, :], agg[:, m, lo:lo + nn]))
            halves.close()
            terms = norm_terms(f"{t}0", layer, 1, stats[0], sc1, sh1, [st])
            for c0 in range(0, NCH, 2):
                chunks = range(c0, min(c0 + 2, NCH))
                lo, hi_end = c0 * CH, min((c0 + 2) * CH, N)
                for m in range(KC):
                    u = act("c_u", [terms], lambda g, m=m, lo=lo, hi_end=hi_end: g.activation(
                        agg[:, m, lo:hi_end], agg[:, m, lo:hi_end], ACT.Relu, bias=sh1[:, m:m + 1],
                        scale=sc1[:, m:m + 1]))
                    for c in chunks:
                        st = dve("c_us", [u], lambda g, m=m, c=c: g.bn_stats(
                            stats[1][:, m, c, :], agg[:, m, c * CH:c * CH + nodes(c)]))
                for c in chunks if store_u else []:
                    u_stored = dma("sync", "u_st", [u], chunk_cols(c), agg[:, :, c * CH:c * CH + nodes(c)])
            if store_u:
                for i in range(WB):
                    w_in[i] = load_ffn_weight(i, [])
                step("sync", stream("fence"), [u_stored], lambda g: g.nop())
            return norm_terms(f"{t}1", layer, 3, stats[1], sc2, sh2, [st])

        aggregate(0)
        with ExitStack() as s:
            w1s, w1_split = split_conv_weight(s, "b_w1", w1[1])
            pH = [ps(s, f"b_ph{i}", [P, TPC, C]) for i in range(2)]
            terms = conv_tail(0, s)
            V = [sb(s, f"b_v{i}", [P, KC, CH]) for i in range(2)]
            VH = [sb(s, f"b_vh{i}", [P, KC, CH], f32r) for i in range(3)]
            VL = [sb(s, f"b_vl{i}", [P, KC, CH], f32r) for i in range(3)]
            H = [sb(s, f"b_h{i}", [P, TPC, C]) for i in range(3)]
            v, vt, prod, biased, hst = {}, {}, {}, {}, {}
            for i in range(NCH + 4):
                q = i
                if q < NCH:
                    nn, lo, b = nodes(q), q * CH, q % 2
                    for m in range(KC):
                        v[q] = act("b_v", [terms, vt.get(q - 2)], lambda g, m=m, nn=nn, lo=lo, b=b: g.activation(
                            V[b][:, m, 0:nn], agg[:, m, lo:lo + nn], ACT.Relu, bias=sh2[:, m:m + 1],
                            scale=sc2[:, m:m + 1]))
                    pool("b_clr", [v[q]], lambda g, lo=lo, nn=nn, q=q: g.memset(
                        agg[:, :, lo:(lo + nn if q < NCH - 1 else AW)], 0.0))
                q = i - 1
                if 0 <= q < NCH:
                    nn, b, b3 = nodes(q), q % 2, q % 3
                    h = dve("b_vh", [v[q], prod.get(q - 3)], lambda g, nn=nn, b=b, b3=b3: g.tensor_copy(
                        VH[b3][:, :, 0:nn], V[b][:, :, 0:nn]))
                    vt[q] = dve("b_vl", [h], lambda g, nn=nn, b=b, b3=b3: g.tensor_tensor(
                        VL[b3][:, :, 0:nn], V[b][:, :, 0:nn], VH[b3][:, :, 0:nn].bitcast(fp32), ALU.subtract))
                q = i - 2
                if 0 <= q < NCH:
                    prod[q] = hidden_product("b", q, passes((VH[q % 3], VL[q % 3]), w1s), pH[q % 2],
                                             [vt[q], w1_split, biased.get(q - 2)])
                q = i - 3
                if 0 <= q < NCH:
                    biased[q], hst[q] = hidden_out("b", q, b1_all[1], H[q % 3], pH[q % 2], h_dram[1],
                                                   [prod[q], hst.get(q - 3)])
            last_stores(hst)
            run_block()

        aggregate(1)
        edges.close()
        with ExitStack() as s:
            conv_tail(1, s, store_u=True)
            dve("seen", list(w_in.values()), lambda g: g.memset(ones_row[0:1, 0:1], 1.0))
            run_block()
        convs.close()

        with ExitStack() as s:
            whi = {n: sb(s, f"{n}_hi", [P, NX, KC, C], f32r) for n in names}
            wlo = {n: sb(s, f"{n}_lo", [P, NX, KC, C], f32r) for n in names}
            wrh, wrl = sb(s, "wrh", [P, KC, P], f32r), sb(s, "wrl", [P, KC, P], f32r)
            scale = [sb(s, f"f_sc{i}", [P, NX * KC]) for i in range(2)]
            shift = [sb(s, f"f_sh{i}", [P, NX * KC]) for i in range(2)]
            x1 = [sb(s, f"f_x{i}", [P, TPC, C]) for i in range(2)]
            xr = sb(s, "f_xr", [P, TPC, C])
            u = sb(s, "f_u", [P, KC, CH])
            y = sb(s, "f_y", [P, TPC, C])
            yhi = [sb(s, f"f_yh{i}", [P, KC, CH], f32r) for i in range(2)]
            ylo = [sb(s, f"f_yl{i}", [P, KC, CH], f32r) for i in range(2)]
            hf = [sb(s, f"f_hf{i}", [P, KC, CH]) for i in range(2)]
            hhi = [[sb(s, f"f_hh{l}{i}", [P, KC, CH], f32r) for i in range(2)] for l in range(2)]
            hlo = [[sb(s, f"f_hl{l}{i}", [P, KC, CH], f32r) for i in range(2)] for l in range(2)]
            ST = sb(s, "f_st", [P, TPC, 6])
            MV = sb(s, "f_mv", [P, TPC, 2])
            lg = sb(s, "f_lg", [P, TPC, NX])
            ex = sb(s, "f_ex", [P, TPC, NX])
            mx = sb(s, "f_mx", [P, TPC])
            sm = sb(s, "f_sm", [P, TPC])
            gate = [sb(s, f"f_gate{i}", [P, TPC, NX]) for i in range(2)]
            lgT = sb(s, "f_lgt", [NX, CH])
            Q = 32
            gT = sb(s, "f_gt", [3 * Q, CH], f32r)
            bo3 = sb(s, "f_bo3", [3 * Q, C], f32r)
            p1 = ps(s, "f_p1", [P, KC, CH])
            p2 = ps(s, "f_p2", [P, KC, CH])
            p3 = ps(s, "f_p3", [P, TPC, C])
            pm = ps(s, "f_pm", [P, KC * CH])

            for l in range(2):
                w = NX * KC
                g_, b_, be_, m_, v_ = (ffn_p[l][:, i * w:(i + 1) * w] for i in range(5))
                t = act("f_sd", [], lambda g, v_=v_: g.activation(v_, v_, ACT.Sqrt, bias=eps_ffn[:, :]))
                t = dve("f_tm", [t], lambda g, v_=v_: g.reciprocal(v_, v_))
                t = dve("f_tm", [t], lambda g, v_=v_, g_=g_, l=l: g.tensor_tensor(scale[l][:, :], v_, g_, ALU.mult))
                t1 = dve("f_tm", [], lambda g, b_=b_, m_=m_: g.tensor_tensor(b_, b_, m_, ALU.subtract))
                t = dve("f_tm", [t1], lambda g, b_=b_, l=l: g.tensor_tensor(b_, b_, scale[l][:, :], ALU.mult))
                terms = dve("f_tm", [t], lambda g, b_=b_, be_=be_, l=l: g.tensor_tensor(shift[l][:, :], b_, be_, ALU.add))
            t = act("f_wr", [], lambda g: g.activation(wrh[:, :, :], wr_raw[:, :, :], ACT.Copy))
            wr_ready = dve("f_wl", [t], lambda g: g.tensor_tensor(
                wrl[:, :, :], wr_raw[:, :, :], wrh[:, :, :].bitcast(fp32), ALU.subtract))

            gT_clear = pool("f_clr", [], lambda g: g.memset(gT[:, :].bitcast(fp32), 0.0))
            bo_clear = pool("f_clr", [], lambda g: g.memset(bo3[:, :].bitcast(fp32), 0.0))
            for q in (0, 2):
                t = act("f_wr", [bo_clear], lambda g, q=q: g.activation(bo3[q * Q:q * Q + NX, :], bo_sb[:, :], ACT.Copy))
            bo_ready = dve("f_wl", [t], lambda g: g.tensor_tensor(
                bo3[Q:Q + NX, :], bo_sb[:, :], bo3[0:NX, :].bitcast(fp32), ALU.subtract))

            w_ready = {}

            def split_weight(i):
                b = i % WB
                n, e = w_order[i]
                hi = act("f_wh", [w_in[i]], lambda g: g.activation(whi[n][:, e, :, :], wst[b][:, :, :], ACT.Copy))
                w_ready[n, e] = dve("f_wl", [hi], lambda g: g.tensor_tensor(
                    wlo[n][:, e, :, :], wst[b][:, :, :], whi[n][:, e, :, :].bitcast(fp32), ALU.subtract))
                if i + WB < len(w_order):
                    w_in[i + WB] = load_ffn_weight(i + WB, [w_ready[n, e]])

            NS = NCH * NX
            y_ready, gate_ready, acc_ready = {}, {}, {}
            l1, l2, l3, h1_ready, h2_ready, p1_free, p2_free, acc, stored = ({} for _ in range(9))
            pend = {}

            def load_rows(c):
                for d, sbuf in rows_of(a["x"], c, xr, False):
                    pend["x", c] = dma("sync", "f_ldx", [pend.get(("x1", c - 1))], d, sbuf)
                pend["u", c] = dma("sync", "f_ldu", [pend.get(("turned", c - 1))], u[:, :, 0:nodes(c)], chunk_cols(c))

            def pre_residual(c):
                b, nn = c % 2, nodes(c)
                for m in range(KC):
                    q = act("f_q", [pend["u", c]], lambda g, m=m: g.activation(
                        u[:, m, 0:nn], u[:, m, 0:nn], ACT.Identity, bias=sh2[:, m:m + 1], scale=sc2[:, m:m + 1]))
                pend["q", c] = q

            def pre_rows(c):
                b = c % 2
                v = pm[:, :].rearrange("p (j n) -> p j n", n=C)
                pend["turned", c] = t = pe("f_t", [pend["q", c], pend.get(("pm", c - 1))],
                                           [tr(v[0:r, j, k * P:(k + 1) * P], u[:, k, j * P:j * P + r], ident[:, :])
                                            for j, r in tiles(c) for k in range(KC)])
                centered = center("f", c, x1[b], xr, ln1[:, c * TPC:(c + 1) * TPC, :],
                                  [pend["x", c], stored.get(c - 2)], TPC)
                for j, r in tiles(c):
                    a1 = dve("f_a", centered + [t], lambda g, j=j, r=r: g.scalar_tensor_tensor(
                        x1[b][0:r, j, :], x1[b][0:r, j, :], ln1[0:r, c * TPC + j, 1:2], v[0:r, j, :], ALU.mult, ALU.add))
                pend["rows", c] = a1
                for j, k, r in groups(c):
                    pend["x1", c] = dve("f_s", [a1], lambda g, j=j, k=k, r=r: g.scalar_tensor_tensor(
                        x1[b][0:r, j:j + k, :], x1[b][0:r, j:j + k, :], 0.0, xr[0:r, j:j + k, :], ALU.max, ALU.add))

            def pre_norm(c):
                sd = row_stats("f", c, x1[c % 2], ST, MV, [pend["x1", c], pend.get(("y", c - 1))])
                rs = row_rstd("f", c, MV, [sd])
                pend["y", c] = normalize("f", c, y, x1[c % 2], MV, [rs, pend.get(("yt", c - 1))])

            def pre_turn(c):
                b, nn = c % 2, nodes(c)
                pend["yt", c] = t = pe("f_yt", [pend["y", c], pend["rows", c]],
                                       [tr(pm[:, k * CH + j * P:k * CH + j * P + r], y[0:r, j, k * P:(k + 1) * P],
                                           ident[0:r, 0:r]) for j, r in tiles(c) for k in range(KC)])
                v = pm[:, :].rearrange("p (k n) -> p k n", k=KC)[:, :, 0:nn]
                h = act("f_yh", [t, l1.get(c * NX - NX - 1)], lambda g: g.activation(yhi[b][:, :, 0:nn], v, ACT.Copy))
                y_ready[c] = dve("f_yl", [h], lambda g: g.tensor_tensor(
                    ylo[b][:, :, 0:nn], v, yhi[b][:, :, 0:nn].bitcast(fp32), ALU.subtract))

            def pre_logits(c):
                b, nn = c % 2, nodes(c)
                pr = passes((yhi[b], ylo[b]), (wrh, wrl))
                t = pe("f_lg", [y_ready[c], wr_ready],
                       [mm(pm[:, 0:nn], w[:, k, :], u[:, k, 0:nn], i == 0 and k == 0, i == 2 and k == KC - 1)
                        for i, (u, w) in enumerate(pr) for k in range(KC)])
                pend["lgt", c] = act("f_lt", [t, pend.get(("lg", c - 1))], lambda g: g.activation(
                    lgT[:, 0:nn], pm[0:NX, 0:nn], ACT.Identity, bias=br_col[:, :]))

            def pre_gate(c):
                b = c % 2
                lgp = pm[:, CH:CH + TPC * NX].rearrange("p (j e) -> p j e", e=NX)
                t = pe("f_lr", [pend["lgt", c]],
                       [tr(lgp[0:r, j, :], lgT[:, j * P:j * P + r], ident[0:NX, 0:NX]) for j, r in tiles(c)])
                for j, k, r in groups(c):
                    t1 = dve("f_g", [t, pend.get(("ex", c - 1))], lambda g, j=j, k=k, r=r: g.tensor_copy(
                        lg[0:r, j:j + k, :], lgp[0:r, j:j + k, :]))
                pend["lg", c] = t1
                for j, k, r in groups(c):
                    t2 = dve("f_g", [t1], lambda g, j=j, k=k, r=r: g.tensor_reduce(
                        mx[0:r, j:j + k], lg[0:r, j:j + k, :], AX.X, ALU.max))
                for j, k, r in groups(c):
                    t3 = dve("f_g", [t2], lambda g, j=j, k=k, r=r: g.tensor_tensor(
                        lg[0:r, j:j + k, :], lg[0:r, j:j + k, :],
                        mx[0:r, j:j + k].unsqueeze(2).broadcast_to([r, k, NX]), ALU.subtract))
                for j, k, r in groups(c):
                    t4 = act("f_ex", [t3, gate_ready.get(c - 1)], lambda g, j=j, k=k, r=r: g.activation(
                        ex[0:r, j:j + k, :], lg[0:r, j:j + k, :], ACT.Exp))
                pend["ex", c] = t4
                for j, k, r in groups(c):
                    t5 = dve("f_g", [t4], lambda g, j=j, k=k, r=r: g.tensor_reduce(
                        sm[0:r, j:j + k], ex[0:r, j:j + k, :], AX.X, ALU.add))
                for j, k, r in groups(c):
                    t6 = dve("f_g", [t5], lambda g, j=j, k=k, r=r: g.reciprocal(sm[0:r, j:j + k], sm[0:r, j:j + k]))
                for j, k, r in groups(c):
                    gate_ready[c] = dve("f_g", [t6], lambda g, j=j, k=k, r=r, b=b: g.tensor_tensor(
                        gate[b][0:r, j:j + k, :], ex[0:r, j:j + k, :],
                        sm[0:r, j:j + k].unsqueeze(2).broadcast_to([r, k, NX]), ALU.mult))

            def pre_bias_turn(c):
                b, nn = c % 2, nodes(c)
                t = pe("f_gt", [gate_ready[c]],
                       [tr(pm[0:NX, CH + j * P:CH + j * P + r], gate[b][0:r, j, :], ident[0:r, 0:r]) for j, r in tiles(c)])
                src = pm[0:NX, CH:CH + nn]
                for q in range(2):
                    h = act("f_ge", [t, gT_clear, pend.get(("bo", c - 1))], lambda g, q=q: g.activation(
                        gT[q * Q:q * Q + NX, 0:nn], src, ACT.Copy))
                pend["gt", c] = dve("f_gl", [h], lambda g: g.tensor_tensor(
                    gT[2 * Q:2 * Q + NX, 0:nn], src, gT[0:NX, 0:nn].bitcast(fp32), ALU.subtract))

            def pre_bias(c):
                b = c % 2
                v = pm[:, :].rearrange("p (j n) -> p j n", n=C)
                pend["bo", c] = t = pe("f_bo", [pend["gt", c], pend["lg", c], bo_ready],
                                       [mm(v[0:r, j, :], gT[:, j * P:j * P + r], bo3[:, :], True, True) for j, r in tiles(c)])
                for j, k, r in groups(c):
                    pend["pm", c] = acc_ready[c] = dve("f_ac", [t], lambda g, j=j, k=k, r=r: g.tensor_tensor(
                        x1[b][0:r, j:j + k, :], v[0:r, j:j + k, :], x1[b][0:r, j:j + k, :], ALU.add))

            def three(w, xh, xl, e, c, o):
                nn = nodes(c)
                pr = [(whi[w], xh), (whi[w], xl), (wlo[w], xh)]
                return [mm(o[:, m, 0:nn], ww[:, e, k, m * P:(m + 1) * P], xx[:, k, 0:nn], i == 0 and k == 0,
                           i == 2 and k == KC - 1)
                        for m in range(KC) for i, (ww, xx) in enumerate(pr) for k in range(KC)]

            def hidden(l, p, prod, i, c, e, reader):
                nn, b = nodes(c), i % 2
                for m in range(KC):
                    col = slice(e * KC + m, e * KC + m + 1)
                    hi = act(f"f_a{l}", [prod, reader, terms], lambda g, m=m, col=col: g.activation(
                        hhi[l][b][:, m, 0:nn], p[:, m, 0:nn], ACT.Relu, bias=shift[l][:, col], scale=scale[l][:, col]))
                for m in range(KC):
                    col = slice(e * KC + m, e * KC + m + 1)
                    full = act(f"f_a{l}", [pend.get(("lo", l))], lambda g, m=m, col=col: g.activation(
                        hf[l][:, m, 0:nn], p[:, m, 0:nn], ACT.Relu, bias=shift[l][:, col], scale=scale[l][:, col]))
                lo = dve(f"f_l{l}", [full], lambda g: g.tensor_tensor(
                    hlo[l][b][:, :, 0:nn], hf[l][:, :, 0:nn], hhi[l][b][:, :, 0:nn].bitcast(fp32), ALU.subtract))
                pend["lo", l] = lo
                return full, lo

            load_rows(0)
            split_weight(0)
            pre_residual(0)
            pre_rows(0)
            pre_norm(0)
            pre_turn(0)
            for n in range(1, len(names)):
                split_weight(n)
            for i in range(NS + 2):
                c, e = divmod(i, NX)
                if i < NS:
                    l1[i] = pe("f_m1", [y_ready[c], w_ready["W1", e], p1_free.get(i - 1)],
                               three("W1", yhi[c % 2], ylo[c % 2], e, c, p1))
                    p1_free[i], h1_ready[i] = hidden(0, p1, l1[i], i, c, e, l2.get(i - 2))
                    if i == 0:
                        pre_logits(0)
                        load_rows(1)
                    if i == 1:
                        pre_gate(0)
                    if i == 2:
                        pre_bias_turn(0)
                        pre_bias(0)
                    if c + 1 < NCH:
                        if e == 3:
                            pre_rows(c + 1)
                        if e == 4:
                            pre_norm(c + 1)
                        if e == 5:
                            pre_turn(c + 1)
                        if e == 6:
                            pre_logits(c + 1)
                        if e == 7:
                            pre_gate(c + 1)
                    if e == 0 and c > 0:
                        pre_bias_turn(c)
                    if e == 1 and c > 0:
                        pre_bias(c)
                    if e == 1 and 0 < c < NCH - 1:
                        load_rows(c + 1)
                    if e == 2 and c + 1 < NCH:
                        pre_residual(c + 1)
                    if c == 0 and e + 1 < NX:
                        for n in range(len(names)):
                            split_weight(len(names) * (e + 1) + n)
                if 1 <= i <= NS:
                    q = i - 1
                    cq, eq = divmod(q, NX)
                    l2[q] = pe("f_m2", [h1_ready[q], w_ready["W2", eq], p2_free.get(q - 1)],
                               three("W2", hhi[0][q % 2], hlo[0][q % 2], eq, cq, p2))
                    p2_free[q], h2_ready[q] = hidden(1, p2, l2[q], q, cq, eq, l3.get(q - 2))
                if i >= 2:
                    q = i - 2
                    cq, eq = divmod(q, NX)
                    b = q % 2
                    pr = [(hhi[1][b], whi["Wo"]), (hhi[1][b], wlo["Wo"]), (hlo[1][b], whi["Wo"])]
                    l3[q] = pe("f_m3", [h2_ready[q], w_ready["Wo", eq], acc.get(q - 1)],
                               [mm(p3[0:r, j, :], xx[:, k, j * P:j * P + r], ww[:, eq, k, :], n == 0 and k == 0,
                                   n == 2 and k == KC - 1)
                                for j, r in tiles(cq) for n, (xx, ww) in enumerate(pr) for k in range(KC)])
                    for j, r in tiles(cq):
                        acc[q] = dve("f_c3", [l3[q], acc_ready[cq] if eq == 0 else acc[q - 1]],
                                     lambda g, j=j, r=r, cq=cq, eq=eq: g.scalar_tensor_tensor(
                                         x1[cq % 2][0:r, j, :], p3[0:r, j, :], gate[cq % 2][0:r, j, eq:eq + 1],
                                         x1[cq % 2][0:r, j, :], ALU.mult, ALU.add))
                    if eq == NX - 1:
                        for d, sbuf in rows_of(out, cq, x1[cq % 2], True):
                            stored[cq] = dma("sync", f"f_st{cq % 2}", [acc[q]], d, sbuf)
            step("sync", stream("fence"), [stored[NCH - 1], stored[NCH - 2]], lambda g: g.nop())
            run_block()


def kernel(**inputs):
    import numpy as np
    import concourse.bacc as bacc
    from concourse import mybir
    from concourse.bass_utils import run_bass_kernel_spmd

    nc = bacc.Bacc("TRN2", target_bir_lowering=False, num_devices=1)
    arrays, aps = {}, {}
    for name, value in inputs.items():
        v = np.ascontiguousarray(value)
        arrays[f"in_{name}"] = v
        aps[name] = nc.dram_tensor(f"in_{name}", v.shape, mybir.dt.from_np(v.dtype), kind="ExternalInput").ap()
    out = nc.dram_tensor("out_x", arrays["in_x"].shape, mybir.dt.float32, kind="ExternalOutput").ap()
    build(nc, aps, out)
    r = run_bass_kernel_spmd(nc, [arrays], core_ids=[0])
    return r.results[0]["out_x"]
```

```python
def build(nc, a, out):
    import concourse.bass as bass
    from concourse import mybir
    from contextlib import ExitStack

    fp32, f32r, i32 = mybir.dt.float32, mybir.dt.float32r, mybir.dt.int32
    ALU, ACT, AX = mybir.AluOpType, mybir.ActivationFunctionType, mybir.AxisListType

    P = 128
    N, C = a["x"].shape
    E = a["src"].shape[0]
    NX = a["L0_ffn_Wr"].shape[1]
    KC = C // P
    TPC = 4
    CH = TPC * P
    NCH = -(-N // CH)
    ET = -(-E // P)
    GT = 4
    GE = GT * P
    NG = -(-E // GE)
    GB = -(-NG // P)
    GW = GB * P
    LN_EPS, BN_EPS, FFN_EPS = 1e-5, 1e-5, 1e-3
    assert C == KC * P and N > P and E > P

    def nodes(c):
        return min(CH, N - c * CH)

    def tiles(c):
        return [(j, min(P, nodes(c) - j * P)) for j in range(-(-nodes(c) // P))]

    def groups(c):
        full, rest = divmod(nodes(c), P)
        return ([(0, full, P)] if full else []) + ([(full, 1, rest)] if rest else [])

    top = ExitStack()

    class Stream:

        def __init__(self, name, by=1):
            self.sem, self.n, self.by = top.enter_context(nc.semaphore(name)), 0, by

    streams = {}

    def stream(name, by=1):
        if name not in streams:
            streams[name] = Stream(name, by)
        return streams[name]

    queues = {e: [] for e in ("sync", "scalar", "vector", "gpsimd", "tensor")}
    waited = {}

    def step(engine, signal, waits, fn):
        need = {}
        for w in waits:
            if w is not None:
                need[w[0]] = max(need.get(w[0], 0), w[1])
        todo = [(s, v) for s, v in need.items() if waited.get((engine, s), 0) < v]
        for s, v in todo:
            waited[(engine, s)] = v
        token = None
        if signal is not None:
            signal.n += signal.by
            token = (signal, signal.n)

        def emit(eng):
            for s, v in todo:
                eng.wait_ge(s.sem, v)
            ins = fn(eng)
            if signal is not None:
                ins.then_inc(signal.sem, signal.by)
        queues[engine].append(emit)
        return token

    entry = {
        "sync": lambda b: b.sync, "scalar": lambda b: b.scalar, "vector": lambda b: b.vector,
        "gpsimd": lambda b: b.gpsimd, "tensor": lambda b: b.tensor,
    }

    def run_block():
        with nc.Block() as block:
            for name in queues:
                def body(eng, todo=list(queues[name])):
                    for emit in todo:
                        emit(eng)
                entry[name](block)(body)
                queues[name].clear()

    def dma(engine, name, waits, dst, src):
        return step(engine, stream(name, 16), waits, lambda g: g.dma_start(dst, src))

    def dve(name, waits, fn):
        return step("vector", stream(name), waits, fn)

    def act(name, waits, fn):
        return step("scalar", stream(name), waits, fn)

    def pool(name, waits, fn):
        return step("gpsimd", stream(name), waits, fn)

    def pe(name, waits, fns):
        def emit(g):
            for f in fns:
                ins = f(g)
            return ins
        return step("tensor", stream(name), waits, emit)

    def mm(o, l, r, start, stop):
        return lambda g: nc.tensor.matmul(o, l, r, start=start, stop=stop)

    def tr(o, i, ident_rows):
        return lambda g: nc.tensor.transpose(o, i, ident_rows)

    def rows_of(dram, c, buf, write):
        for j, k, r in groups(c):
            lo = c * CH + j * P
            d = dram[lo:lo + k * r, :].rearrange("(k p) n -> p k n", p=r)
            s = buf[0:r, j:j + k, :]
            yield (d, s) if write else (s, d)

    with top:
        def sb(ctx, name, shape, dt=fp32):
            return ctx.enter_context(nc.sbuf_tensor(name, shape, dt))

        def ps(ctx, name, shape):
            return ctx.enter_context(nc.psum_tensor(name, shape, fp32))

        h_dram = [nc.dram_tensor(f"h{i}", (N, C), fp32, kind="Internal").ap() for i in range(2)]
        u_dram = nc.dram_tensor("u", (NCH, P, KC * CH), fp32, kind="Internal").ap()
        base_dram = nc.dram_tensor("group_base", (GB, P), i32, kind="Internal").ap()

        ident = sb(top, "ident", [P, P])
        eps_ln = sb(top, "eps_ln", [P, 1])
        eps_ffn = sb(top, "eps_ffn", [P, 1])
        ones_row = sb(top, "ones_row", [1, P])
        ln1 = sb(top, "ln1", [P, NCH * TPC, 3])
        conv_p = sb(top, "conv_p", [P, 10 * KC])
        ffn_p = [sb(top, f"ffn_p{i}", [P, 5 * NX * KC]) for i in range(2)]
        wr_raw = sb(top, "wr_raw", [P, KC, P])
        br_col = sb(top, "br_col", [NX, 1])
        bo_sb = sb(top, "bo_sb", [NX, C])

        conv_names = [f"L0_gnn_{n}" for c in "12" for n in (f"c{c}_b2", f"c{c}_g", f"c{c}_b", f"bn{c}_g", f"bn{c}_b")]

        def conv_cols(layer, which):
            i = KC * (5 * layer + which)
            return conv_p[:, i:i + KC]

        sc2, sh2 = sb(top, "sc2", [P, KC]), sb(top, "sh2", [P, KC])
        WB = 4
        wst = [sb(top, f"wst{i}", [P, KC, C]) for i in range(WB)]

        xr = sb(top, "f_xr", [P, TPC, C])
        u = sb(top, "f_u", [P, KC, CH])

        names = ("W1", "W2", "Wo")
        w_order = [(n, e) for e in range(NX) for n in names]

        def load_ffn_weight(i, waits):
            n, e = w_order[i]
            return dma("sync", f"f_wld{i % WB}", waits, wst[i % WB][:, :, :],
                       a[f"L0_ffn_{n}"][e].rearrange("(k p) n -> p k n", p=P))

        convs = ExitStack()
        w1 = [sb(convs, f"w1_{i}", [P, KC, C]) for i in range(2)]
        w2 = [sb(convs, f"w2_{i}", [P, KC, C]) for i in range(2)]
        b1_all = [sb(convs, f"b1_{i}", [P, C]) for i in range(2)]
        AW = N + P
        agg = sb(convs, "agg", [P, KC, AW])
        z_stats = sb(convs, "z_stats", [P, KC, NCH, 6])
        edges = ExitStack()
        src_col = sb(edges, "src_col", [P, GT * GW], i32)
        rel_col = sb(edges, "rel_col", [P, GT * GW])
        ew_col = sb(edges, "ew_col", [P, GT * GW])
        base_row = sb(edges, "base_row", [1, GW], i32)
        lane = sb(edges, "lane", [P, P])
        far = sb(edges, "far", [1, 1], i32)
        whole_row = sb(edges, "whole_row", [1, GW], i32)

        aggregated = {}

        def row_stats(tag, c, x, stats, mv, waits):
            for j, r in tiles(c):
                t = dve(f"{tag}_st", waits, lambda g, j=j, r=r: g.bn_stats(stats[0:r, j, :], x[0:r, j, :]))
            for j, r in tiles(c):
                t2 = dve(f"{tag}_ag", [t], lambda g, j=j, r=r: g.bn_aggr(mv[0:r, j, 0:2], stats[0:r, j, :]))
            aggregated[tag, c] = t2
            for j, k, r in groups(c):
                t3 = act(f"{tag}_sd", [t2], lambda g, j=j, k=k, r=r: g.activation(
                    mv[0:r, j:j + k, 1], mv[0:r, j:j + k, 1], ACT.Sqrt, bias=eps_ln[0:r, :]))
            return t3

        def row_rstd(tag, c, mv, waits):
            for j, k, r in groups(c):
                t = dve(f"{tag}_rs", waits, lambda g, j=j, k=k, r=r: g.reciprocal(
                    mv[0:r, j:j + k, 1], mv[0:r, j:j + k, 1]))
            return t

        def row_minus_mean(tag, c, mv, waits):
            for j, k, r in groups(c):
                t = dve(f"{tag}_mm", waits, lambda g, j=j, k=k, r=r: g.tensor_scalar(
                    mv[0:r, j:j + k, 2], mv[0:r, j:j + k, 0], -1.0, None, ALU.mult))
            return t

        def center(tag, c, dst, x, mv, waits, on_vector):
            last = {}
            for j, r in tiles(c):
                if j >= TPC - on_vector:
                    last["v"] = dve(f"{tag}_cv", waits, lambda g, j=j, r=r: g.tensor_scalar(
                        dst[0:r, j, :], x[0:r, j, :], mv[0:r, j, 0:1], None, ALU.subtract))
                else:
                    last["a"] = act(f"{tag}_ca", waits, lambda g, j=j, r=r: g.activation(
                        dst[0:r, j, :], x[0:r, j, :], ACT.Identity, bias=mv[0:r, j, 2:3]))
            return list(last.values())

        def normalize(tag, c, dst, x, mv, waits):
            for j, r in tiles(c):
                t = step("vector", stream(f"{tag}_nm"), waits, lambda g, j=j, r=r: g.tensor_scalar(
                    dst[0:r, j, :], x[0:r, j, :], mv[0:r, j, 0:1], mv[0:r, j, 1:2], ALU.subtract, ALU.mult))
            return t

        def passes(x, w):
            return [(x[0], w[0]), (x[0], w[1]), (x[1], w[0])]

        def split_conv_weight(s, name, w):
            hi, lo = sb(s, f"{name}_hi", [P, KC, C], f32r), sb(s, f"{name}_lo", [P, KC, C], f32r)
            t = act("w_hi", [], lambda g: g.activation(hi[:, :, :], w[:, :, :], ACT.Copy))
            return (hi, lo), dve("w_lo", [t], lambda g: g.tensor_tensor(
                lo[:, :, :], w[:, :, :], hi[:, :, :].bitcast(fp32), ALU.subtract))

        def hidden_product(tag, c, pairs, pH, waits):
            return pe(f"{tag}_h", waits,
                      [mm(pH[0:r, j, :], x[:, k, j * P:j * P + r], w[:, k, :], n == 0 and k == 0,
                          n == len(pairs) - 1 and k == KC - 1)
                       for j, r in tiles(c) for n, (x, w) in enumerate(pairs) for k in range(KC)])

        def hidden_out(tag, c, bias, hbuf, pH, h_out, waits, rstd=None):
            for j, r in tiles(c) if rstd is not None else []:
                biased = dve(f"{tag}_hb", waits, lambda g, j=j, r=r: g.scalar_tensor_tensor(
                    hbuf[0:r, j, :], pH[0:r, j, :], rstd[0:r, j, :], bias[0:r, :], ALU.mult, ALU.add))
            for j, k, r in groups(c) if rstd is None else []:
                biased = dve(f"{tag}_hb", waits, lambda g, j=j, k=k, r=r: g.tensor_tensor(
                    hbuf[0:r, j:j + k, :], pH[0:r, j:j + k, :],
                    bias[0:r, :].unsqueeze(1).broadcast_to([r, k, C]), ALU.add))
            for j, k, r in groups(c):
                v = hbuf[0:r, j:j + k, :]
                relu = act(f"{tag}_hr", [biased], lambda g, v=v: g.activation(v, v, ACT.Relu))
            for d, sbuf in rows_of(h_out, c, hbuf, True):
                st = dma("sync", f"{tag}_hst{c % 3}", [relu], d, sbuf)
            return biased, st

        def last_stores(stored):
            step("sync", stream("fence"), [stored[c] for c in range(max(0, NCH - 3), NCH)], lambda g: g.nop())

        with ExitStack() as s:
            def in_agg(i, dt=fp32):
                v = agg[:, 0, i * GB * GE:(i + 1) * GB * GE]
                return (v if dt == fp32 else v.bitcast(dt)).rearrange("p (b e) -> p b e", e=GE)
            assert 5 * GB * GE <= AW
            raw = {"src": in_agg(0, i32), "dst": in_agg(1, i32), "ew": in_agg(2)}
            src_f, dst_f = in_agg(3), in_agg(4)
            group_min = sb(s, "group_min", [P, GB])
            group_max = sb(s, "group_max", [P, GB])
            span = sb(s, "span", [P, 1])
            base_i = sb(s, "base_i", [GB, P], i32)
            prow = [sb(s, f"prow{i}", [P, P]) for i in range(3)]
            brow = sb(s, "brow", [1, 2 * C])
            base_f, rise = sb(s, "base_f", [1, GW]), sb(s, "rise", [1, GW])
            ordered, narrow = sb(s, "ordered", [1, 1]), sb(s, "narrow", [1, 1])
            X = [sb(s, f"a_x{i}", [P, TPC, C]) for i in range(3)]
            Y = [sb(s, f"a_y{i}", [P, TPC, C]) for i in range(2)]
            YT = [sb(s, f"a_yt{i}", [P, KC, CH]) for i in range(2)]
            H = [sb(s, f"a_h{i}", [P, TPC, C]) for i in range(3)]
            ST = [sb(s, f"a_st{i}", [P, TPC, 6]) for i in range(2)]
            pT = [ps(s, f"a_pt{i}", [P, KC * CH]) for i in range(2)]
            pH = [ps(s, f"a_ph{i}", [P, TPC, C]) for i in range(2)]
            pT_free, pH_free = [[], []], [[], []]

            zi = pool("init", [], lambda g: g.memset(ident[:, :], 0.0))
            ident_ready = pool("init", [zi], lambda g: g.affine_select(
                out=ident[:, :], in_=ident[:, :], compare_op=ALU.not_equal, fill=1.0, base=0,
                pattern=[[-1, P]], channel_multiplier=1))
            pool("init", [], lambda g: g.memset(eps_ln[:, :], LN_EPS))
            eps_ready = pool("init", [], lambda g: g.memset(eps_ffn[:, :], FFN_EPS))
            wr_clear = pool("init", [], lambda g: g.memset(wr_raw[:, :, :], 0.0))
            ones_ready = pool("init", [], lambda g: g.memset(ones_row[:, :], 1.0))
            pool("init", [], lambda g: g.iota(lane[:, :], pattern=[[1, P]], base=0, channel_multiplier=0,
                                              allow_small_or_imprecise_dtypes=True))

            def load_x(c):
                for d, sbuf in rows_of(a["x"], c, X[c % 3], False):
                    ld = dma("sync", f"a_ld{c % 3}", normed.get(c - 3, []), d, sbuf)
                return ld

            normed, turned, evac, prod, hst, x_in, sd, minus, rstd = ({} for _ in range(9))
            for c in range(2):
                x_in[c] = load_x(c)

            for i, (n, l) in enumerate((("w1", 0), ("w1", 1), ("w2", 0), ("w2", 1))):
                w = (w1 if n == "w1" else w2)[l]
                t = dma("scalar", f"ld_w{i > 0}", [], w[:, :, :],
                        a[f"L0_gnn_c{l + 1}_{n}"].rearrange("(k p) n -> p k n", p=P))
                if i == 0:
                    w1_loaded = t
                    for layer in range(2):
                        dma("scalar", "ld_bias", [], brow[0:1, layer * C:(layer + 1) * C],
                            a[f"L0_gnn_c{layer + 1}_b1"].rearrange("(p n) -> p n", p=1))
                    bias_loaded = dma("scalar", "ld_bias", [], br_col[:, :],
                                      a["L0_ffn_br"].rearrange("(p n) -> p n", n=1))
            weights_loaded = t

            for r in raw.values():
                cleared = dve("clear", [], lambda g, r=r: g.memset(r[:, GB - 1, :], 0))
            loaded = {}
            full_blocks, last_groups, last_edges = NG // P, E // GE - (NG // P) * P, E % GE
            for n, dram in (("src", a["src"]), ("dst", a["dst"]), ("ew", a["edge_weight"])):
                lo = full_blocks * P * GE
                t = dma("gpsimd", f"ld_{n}", [], raw[n][:, 0:full_blocks, :],
                        dram[0:lo].rearrange("(b p e) -> p b e", p=P, e=GE))
                if last_groups:
                    t = dma("gpsimd", f"ld_{n}", [cleared], raw[n][0:last_groups, GB - 1, :],
                            dram[lo:lo + last_groups * GE].rearrange("(p e) -> p e", e=GE))
                if last_edges:
                    lo += last_groups * GE
                    t = dma("gpsimd", f"ld_{n}", [cleared],
                            raw[n][last_groups:last_groups + 1, GB - 1, 0:last_edges],
                            dram[lo:E].rearrange("(p e) -> p e", p=1))
                    if n == "dst":
                        need = GE - last_edges
                        t = dma("gpsimd", f"ld_{n}", [],
                                raw[n][last_groups:last_groups + 1, GB - 1, last_edges:GE],
                                dram[E - need:E].rearrange("(p e) -> p e", p=1))
                loaded[n] = t

            dma("gpsimd", "ld_par", [], bo_sb[:, :], a["L0_ffn_bo"])
            dma("gpsimd", "ld_par", [wr_clear], wr_raw[:, :, 0:NX], a["L0_ffn_Wr"].rearrange("(k p) n -> p k n", p=P))
            for i, n in enumerate(conv_names):
                dma("gpsimd", "ld_par", [], prow[2][KC * i:KC * (i + 1), :], a[n].rearrange("(m p) -> m p", p=P))
            for layer in range(2):
                for i, n in enumerate(("g", "b", "be", "m", "v")):
                    w = NX * KC
                    params = dma("gpsimd", "ld_par", [], prow[layer][w * i:w * (i + 1), :],
                                 a[f"L0_ffn_{n}{layer + 1}"].rearrange("e (m p) -> (e m) p", p=P))

            done = {}

            def side_params(b):
                cols = [0, P, 2 * P]
                turned_p = pe("p_par", [params, ident_ready] + pT_free[b],
                              [tr(pT[b][:, i * P:i * P + w], prow[i][0:w, :], ident[0:w, 0:w])
                               for i, w in enumerate((5 * NX * KC, 5 * NX * KC, 10 * KC))])
                for i, (dst, w) in enumerate(((ffn_p[0], 5 * NX * KC), (ffn_p[1], 5 * NX * KC), (conv_p, 10 * KC))):
                    t = dve("v_par", [turned_p], lambda g, dst=dst, i=i, w=w: g.tensor_copy(
                        dst[:, :], pT[b][:, i * P:i * P + w]))
                pT_free[b] = [t]

            def side_index(b):
                done["src"] = dve("v_idx", [loaded["src"], cleared], lambda g: g.tensor_copy(src_f[:, :, :], raw["src"][:, :, :]))
                c_dst = dve("v_idx", [loaded["dst"]], lambda g: g.tensor_copy(dst_f[:, :, :], raw["dst"][:, :, :]))
                done["min"] = dve("v_idx", [c_dst], lambda g: g.tensor_reduce(group_min[:, :], dst_f[:, :, :], AX.X, ALU.min))
                done["max"] = dve("v_idx", [c_dst], lambda g: g.tensor_reduce(group_max[:, :], dst_f[:, :, :], AX.X, ALU.max))

            def side_rel(b):
                for e in range(GB):
                    done["dst"] = dve("v_idx", [done["min"]], lambda g, e=e: g.tensor_scalar(
                        dst_f[:, e, :], dst_f[:, e, :], group_min[:, e:e + 1], None, ALU.subtract))
                m = dve("v_idx", [done["max"]], lambda g: g.tensor_tensor(group_max[:, :], group_max[:, :], group_min[:, :], ALU.subtract))
                done["span"] = dve("v_idx", [m], lambda g: g.tensor_reduce(span[:, :], group_max[:, :], AX.X, ALU.max))

            def side_base(b):
                m = pe("p_idx", [done["span"], ident_ready] + pT_free[b],
                       [tr(pT[b][0:1, 0:P], span[:, :], ident[:, :]),
                        tr(pT[b][0:GB, P:2 * P], group_min[:, :], ident[:, :])])
                base_ready = dve("v_idx", [m], lambda g: g.tensor_copy(base_i[:, :], pT[b][0:GB, P:2 * P]))
                m = dve("v_idx", [m], lambda g: g.tensor_reduce(span[0:1, :], pT[b][0:1, 0:P], AX.X, ALU.max))
                pT_free[b] = [m]
                m = dve("v_idx", [m], lambda g: g.tensor_copy(far[:, :], span[0:1, :]))
                m = dve("v_idx", [m], lambda g: g.tensor_single_scalar(
                    far[:, :], far[:, :], P.bit_length() - 1, ALU.arith_shift_right))
                stored = dma("scalar", "st_base", [base_ready], base_dram, base_i[:, :])
                done["base"] = dma("scalar", "ld_base", [stored], base_row[:, :],
                                   base_dram.rearrange("(o b) p -> o (b p)", o=1))

            def side_whole(b):
                v = lambda waits, fn: dve("v_idx", waits, fn)
                t = v([done["base"]], lambda g: g.tensor_copy(base_f[:, 0:NG], base_row[:, 0:NG]))
                t = v([t], lambda g: g.tensor_tensor(rise[:, 0:NG - 1], base_f[:, 1:NG], base_f[:, 0:NG - 1], ALU.subtract))
                t = v([t], lambda g: g.tensor_reduce(ordered[:, :], rise[:, 0:NG - 1], AX.X, ALU.min))
                t = v([t], lambda g: g.tensor_single_scalar(ordered[:, :], ordered[:, :], 0.0, ALU.is_ge))
                t1 = v([t], lambda g: g.tensor_copy(narrow[:, :], far[:, :]))
                t1 = v([t1], lambda g: g.tensor_single_scalar(narrow[:, :], narrow[:, :], 0.0, ALU.is_equal))
                t1 = v([t1], lambda g: g.tensor_tensor(narrow[:, :], narrow[:, :], ordered[:, :], ALU.mult))
                t = v([t], lambda g: g.tensor_single_scalar(
                    whole_row[:, 0:NG], base_row[:, 0:NG], CH.bit_length() - 1, ALU.arith_shift_right))
                t = v([t], lambda g: g.tensor_copy(base_f[:, 0:NG], whole_row[:, 0:NG]))
                t = v([t, t1], lambda g: g.tensor_scalar(
                    base_f[:, 0:NG], base_f[:, 0:NG], float(NCH - 2), narrow[:, :], ALU.min, ALU.mult))
                v([t], lambda g: g.tensor_copy(whole_row[:, 0:NG], base_f[:, 0:NG]))

            def side_turn(srcbuf, dstbuf, key, blocks):
                def go(b):
                    ready = done[key] if key in done else loaded[key]
                    t = pe("p_idx", [ready, cleared, ident_ready] + pT_free[b],
                           [tr(pT[b][:, i * P:(i + 1) * P], srcbuf[:, gb, j * P:(j + 1) * P], ident[:, :])
                            for i, (gb, j) in enumerate((gb, j) for gb in blocks for j in range(GT))])
                    for i, gb in enumerate(blocks):
                        dst = dstbuf[:, :].rearrange("p (j q) -> p j q", q=GW)[:, :, gb * P:(gb + 1) * P]
                        src = pT[b][:, i * GE:(i + 1) * GE].rearrange("p (j q) -> p j q", q=P)
                        t = act("v_turn", [t], lambda g, dst=dst, src=src: g.activation(dst, src, ACT.Copy))
                    pT_free[b] = [t]
                    done["turn"] = t
                return go

            def side_clear(b):
                for k in range(KC):
                    pool("clear_agg", [done["turn"]], lambda g, k=k: g.memset(agg[:, k, :], 0.0))

            side = [side_index, side_rel, side_base]
            per = (KC * CH) // GE
            for lo in range(0, GB, per):
                for srcbuf, dstbuf, key in ((src_f, src_col, "src"), (raw["ew"], ew_col, "ew"), (dst_f, rel_col, "dst")):
                    side.append(side_turn(srcbuf, dstbuf, key, list(range(lo, min(lo + per, GB)))))
            side += [side_whole, side_clear, side_params]

            def spread_biases():
                flat = pH[1][:, :, :].rearrange("p j n -> p (j n)")
                t = pe("p_par", [ones_ready, bias_loaded],
                       [mm(flat[:, l * C:(l + 1) * C], ones_row[:, :], brow[0:1, l * C:(l + 1) * C], True, True)
                        for l in range(2)])
                for l in range(2):
                    t1 = dve("v_bias", [t], lambda g, l=l: g.tensor_copy(b1_all[l][:, :], flat[:, l * C:(l + 1) * C]))
                pH_free[1] = [t1]
                return t1

            def mv_of(c):
                return ln1[:, c * TPC:(c + 1) * TPC, :]

            for i in range(NCH + 4):
                q = i - 2
                if 0 <= q < NCH:
                    b, nn = q % 2, nodes(q)
                    turned[q] = pe("a_t", normed[q] + [ident_ready] + pT_free[b],
                                   [tr(pT[b][:, k * CH + j * P:k * CH + j * P + r], Y[b][0:r, j, k * P:(k + 1) * P],
                                       ident[0:r, 0:r]) for j, r in tiles(q) for k in range(KC)])
                    evac[q] = act("a_ev", [turned[q], prod.get(q - 2)], lambda g, b=b, nn=nn: g.activation(
                        YT[b][:, :, 0:nn], pT[b][:, :].rearrange("p (k n) -> p k n", k=KC)[:, :, 0:nn], ACT.Copy))
                    pT_free[b] = [evac[q]]
                q = i - 3
                if 0 <= q < NCH:
                    prod[q] = hidden_product("a", q, [(YT[q % 2], w1[0])], pH[q % 2],
                                             [evac[q], w1_loaded] + pH_free[q % 2])
                q = i - 1
                if 0 <= q < NCH:
                    normed[q] = center("a", q, Y[q % 2], X[q % 3], mv_of(q), [minus[q], turned.get(q - 2)], 1)
                    rstd[q] = row_rstd("a", q, mv_of(q), [sd[q]])
                q = i - 4
                if 0 <= q < NCH:
                    biased, hst[q] = hidden_out("a", q, b1_all[0], H[q % 3], pH[q % 2], h_dram[0],
                                                [prod[q], bias_ready, rstd[q], hst.get(q - 3)], mv_of(q)[:, :, 1:2])
                    pH_free[q % 2] = [biased]
                q = i
                if q < NCH:
                    sd[q] = row_stats("a", q, X[q % 3], ST[q % 2], mv_of(q), [x_in[q], eps_ready])
                    minus[q] = row_minus_mean("a", q, mv_of(q), [aggregated["a", q]])
                    if q + 2 < NCH:
                        x_in[q + 2] = load_x(q + 2)
                if i == 1:
                    bias_ready = spread_biases()
                if i >= 5 and side:
                    side.pop(0)((i - 2) % 2 if i - 2 >= NCH else (i - 1) % 2)
            assert not side
            last_stores(hst)
            dve("seen", [done["base"], weights_loaded, params], lambda g: g.memset(base_i[0:1, 0:1], 0))
            run_block()

        def aggregate(layer):
            R, RO, AHEAD = 10, 10, 4
            with ExitStack() as s:
                w2s, w2_split = split_conv_weight(s, f"g{layer}_w2", w2[layer])
                G = [sb(s, f"g{layer}_{i}", [P, C]) for i in range(R)]
                OH = [sb(s, f"oh{layer}_{i}", [P, P]) for i in range(RO)]
                SH = [sb(s, f"sh{layer}_{i}", [P, KC, P], f32r) for i in range(2)]
                SL = [sb(s, f"sl{layer}_{i}", [P, KC, P], f32r) for i in range(2)]
                pS = [ps(s, f"ps{layer}_{i}", [P, KC, CH]) for i in range(2)]
                pZ = [ps(s, f"pz{layer}_{i}", [P, CH]) for i in range(2)]
                tile_sums, sums, hi, cut, prod, added = ({} for _ in range(6))
                onehots = []
                BATCH = 16
                regs = {}

                def onehot(e):
                    col = e % GT * GW + e // GT
                    return dve("g_oh", [tile_sums.get(e - RO)], lambda g: g.tensor_scalar(
                        OH[e % RO][:, :], lane[:, :], rel_col[:, col:col + 1], ew_col[:, col:col + 1],
                        ALU.is_equal, ALU.mult))

                def add(g, q):
                    if q % BATCH == 0:
                        if not regs:
                            regs["r"] = [g.alloc_register(f"g{layer}_base{i}") for i in range(BATCH)]
                        k = min(BATCH, NG - q)
                        g.load(regs["r"][0:k], base_row[0:1, q:q + k])
                    base = g.snap(regs["r"][q % BATCH], min_val=0, max_val=N - 1)
                    win = agg[:, :, bass.ds(base, P)]
                    return g.tensor_tensor(win, win, pZ[q % 2][:, 0:KC * P].rearrange("p (k n) -> p k n", k=KC), ALU.add)

                counted = {}

                def count_from_none(g):
                    counted["chunk"] = g.alloc_register(f"g{layer}_chunk")
                    counted["whole"] = g.alloc_register(f"g{layer}_whole")
                    g.reg_mov(counted["chunk"], 0)
                    return g.nop()

                def chunk_stats(g, chunk, m):
                    return g.bn_stats(z_stats[:, m, bass.ds(chunk, 1), :].rearrange("p c s -> p (c s)"),
                                      agg[:, m, bass.ds(chunk * CH, CH)])

                def next_chunk(g, q, m):
                    if m == 0:
                        counted["now"] = g.snap(counted["chunk"], min_val=0, max_val=NCH - 2)
                    ins = chunk_stats(g, counted["now"], m)
                    if m == KC - 1:
                        g.load([counted["whole"]], whole_row[0:1, q:q + 1])
                        g.reg_add(counted["chunk"], counted["chunk"], 1)
                        g.reg_alu(counted["chunk"], counted["chunk"], counted["whole"], ALU.min)
                    return ins

                step("vector", None, [], count_from_none)
                for q in range(NG + 1):
                    for j in range(GT):
                        e, col = q * GT + j, j * GW + q
                        if e < ET:
                            gathered = step("gpsimd", stream(f"g_ga{e % R}", 16), [tile_sums.get(e - R)],
                                            lambda g, e=e, col=col: g.indirect_dma_start(
                                                G[e % R][:, :], None, h_dram[layer],
                                                bass.IndirectOffsetOnAxis(ap=src_col[:, col:col + 1], axis=0)))
                            while len(onehots) < min(e + 1 + AHEAD, ET):
                                onehots.append(onehot(len(onehots)))
                            last = j == GT - 1 or e == ET - 1
                            tile_sums[e] = sums[q] = pe(
                                "g_mm", [gathered, onehots[e], cut.get(q - 2)],
                                [mm(pS[q % 2][:, k, 0:P], G[e % R][:, k * P:(k + 1) * P], OH[e % RO][:, :], j == 0, last)
                                 for k in range(KC)])
                        p = q - 1
                        if j == 0 and p >= 0:
                            v = pS[p % 2][:, :, 0:P]
                            hi[p] = act("g_hi", [sums[p], prod.get(p - 2)], lambda g, p=p, v=v: g.activation(
                                SH[p % 2][:, :, :], v, ACT.Copy))
                            cut[p] = dve("g_lo", [hi[p]], lambda g, p=p, v=v: g.tensor_tensor(
                                SL[p % 2][:, :, :], v, SH[p % 2][:, :, :].bitcast(fp32), ALU.subtract))
                        if j == 2 and p >= 0:
                            prod[p] = pe("g_z", [cut[p], w2_split, added.get(p - 2)],
                                         [mm(pZ[p % 2][:, m * P:(m + 1) * P], w[:, k, m * P:(m + 1) * P], x[:, k, :],
                                             n == 0 and k == 0, n == 2 and k == KC - 1)
                                          for m in range(KC)
                                          for n, (x, w) in enumerate(passes((SH[p % 2], SL[p % 2]), w2s))
                                          for k in range(KC)])
                        if j == 3 and p >= 0:
                            added[p] = dve("g_add", [prod[p], added.get(p - 1)], lambda g, p=p: add(g, p))
                            if p % 4 == 3 and p + 1 < NG:
                                for m in range(KC):
                                    z_st = dve("g_st", [added[p]], lambda g, p=p, m=m: next_chunk(g, p + 1, m))
                far_windows(layer, s, G[0], OH[0], SH[0], SL[0], pS[0], pZ[0], w2s)

                def other_chunks(g):
                    first = g.snap(counted["chunk"], min_val=0, max_val=NCH - 2)
                    left = g.alloc_register(f"g{layer}_left")
                    g.reg_mov(left, NCH - 1)
                    g.reg_alu(left, left, counted["chunk"], ALU.subtract)
                    with g.Fori(0, left) as c:
                        for m in range(KC):
                            chunk_stats(g, g.snap(first + c, min_val=0, max_val=NCH - 2), m)
                    return g.nop()

                step("vector", None, [added[NG - 1]], other_chunks)
                for m in range(KC):
                    dve("g_st", [added[NG - 1]], lambda g, m=m: g.bn_stats(
                        z_stats[:, m, NCH - 1, :], agg[:, m, (NCH - 1) * CH:N]))
                run_block()

        far_sem = {n: top.enter_context(nc.semaphore(f"far_{n}"))
                   for n in ("idx", "gathered", "landed", "onehot", "sums", "cut", "prod", "added", "fixed")}

        def far_windows(layer, s, G, OH, SH, SL, pS, pZ, w2s):
            t = f"x{layer}"
            idx = sb(s, f"{t}_idx", [P, 1], i32)
            rel_w = sb(s, f"{t}_rel", [P, GT * GW])
            rel_e, ew_e = sb(s, f"{t}_rel_e", [P, 1]), sb(s, f"{t}_ew_e", [P, 1])
            base_f = sb(s, f"{t}_base_f", [1, GW])
            base_w = sb(s, f"{t}_base_w", [1, GW], i32)
            sem = far_sem

            def take(g, name):
                g.wait_ge(sem[name], 1)
                g.sem_clear(sem[name])

            def turns(g, start=None, window=None, tile=None):
                count = g.alloc_register(f"{t}_far")
                g.load(count, far[0:1, 0:1])
                with g.If_ne(count, 0):
                    if start:
                        start()
                    with g.Fori(0, count):
                        if window:
                            window()
                        with g.Fori(0, NG) as q:
                            for j in range(GT):
                                tile(q, j)
                return g.nop()

            def pool_loop(g):
                def tile(q, j):
                    g.tensor_copy(idx[:, :], src_col[:, bass.ds(q + j * GW, 1)]).then_inc(sem["idx"], 1)
                    take(g, "idx")
                    g.indirect_dma_start(G[:, :], None, h_dram[layer], bass.IndirectOffsetOnAxis(
                        ap=idx[:, :], axis=0)).then_inc(sem["gathered"], 16)
                    g.wait_ge(sem["gathered"], 16)
                    g.dma_reset(range(sem["gathered"].num, sem["gathered"].num + 1))
                    g.sem_clear(sem["gathered"])
                    g.sem_inc(sem["landed"], 1)
                    take(g, "added")
                return turns(g, tile=tile)

            def pe_loop(g):
                def tile(q, j):
                    take(g, "landed")
                    take(g, "onehot")
                    for k in range(KC):
                        ins = nc.tensor.matmul(pS[:, k, 0:P], G[:, k * P:(k + 1) * P], OH[:, :], start=True, stop=True)
                    ins.then_inc(sem["sums"], 1)
                    take(g, "cut")
                    for m in range(KC):
                        for n, (x, w) in enumerate(passes((SH, SL), w2s)):
                            for k in range(KC):
                                ins = nc.tensor.matmul(
                                    pZ[:, m * P:(m + 1) * P], w[:, k, m * P:(m + 1) * P], x[:, k, :],
                                    start=n == 0 and k == 0, stop=n == 2 and k == KC - 1)
                    ins.then_inc(sem["prod"], 1)
                return turns(g, tile=tile)

            def dve_loop(g):
                def done(ins):
                    ins.then_inc(sem["fixed"], 1)
                    take(g, "fixed")

                def start():
                    done(g.tensor_copy(rel_w[:, :], rel_col[:, :]))
                    done(g.tensor_copy(base_f[:, :], base_row[:, :]))

                def window():
                    done(g.tensor_scalar(rel_w[:, :], rel_w[:, :], float(P), None, ALU.subtract))
                    done(g.tensor_scalar(base_f[:, :], base_f[:, :], float(P), float(N), ALU.add, ALU.min))
                    done(g.tensor_copy(base_w[:, :], base_f[:, :]))

                def tile(q, j):
                    done(g.tensor_copy(rel_e[:, :], rel_w[:, bass.ds(q + j * GW, 1)]))
                    done(g.tensor_copy(ew_e[:, :], ew_col[:, bass.ds(q + j * GW, 1)]))
                    g.tensor_scalar(OH[:, :], lane[:, :], rel_e[:, :], ew_e[:, :], ALU.is_equal,
                                    ALU.mult).then_inc(sem["onehot"], 1)
                    base = g.value_load(base_w[0:1, bass.ds(q, 1)], min_val=0, max_val=N)
                    take(g, "sums")
                    done(g.tensor_copy(SH[:, :, :], pS[:, :, 0:P]))
                    g.tensor_tensor(SL[:, :, :], pS[:, :, 0:P], SH[:, :, :].bitcast(fp32),
                                    ALU.subtract).then_inc(sem["cut"], 1)
                    take(g, "prod")
                    win = agg[:, :, bass.ds(base, P)]
                    done(g.tensor_tensor(win, win, pZ[:, 0:KC * P].rearrange("p (k n) -> p k n", k=KC), ALU.add))
                    g.sem_inc(sem["added"], 1)
                return turns(g, start, window, tile)

            last_add, last_sum, last_prod = stream("g_add"), stream("g_mm"), stream("g_z")
            done_add, done_sum, done_prod = ((x, x.n) for x in (last_add, last_sum, last_prod))
            step("gpsimd", None, [done_sum], pool_loop)
            step("vector", None, [done_add, done_sum, done_prod], dve_loop)
            step("tensor", None, [done_add], pe_loop)

        def norm_terms(tag, layer, which, stats, scale, shift, waits, b2=None):
            mv = tag_mv[tag]
            for m in range(KC):
                t = dve("bn_ag", waits, lambda g, m=m: g.bn_aggr(
                    mv[:, m, :], stats[:, m, :, :].rearrange("p c s -> p (c s)")))
            if b2 is not None:
                t = dve("bn_tm", [t], lambda g: g.tensor_tensor(mv[:, :, 0], mv[:, :, 0], b2, ALU.add))
            t = act("bn_sd", [t], lambda g: g.activation(mv[:, :, 1], mv[:, :, 1], ACT.Sqrt, bias=eps_ln[:, :]))
            t = dve("bn_tm", [t], lambda g: g.reciprocal(mv[:, :, 1], mv[:, :, 1]))
            t = dve("bn_tm", [t], lambda g: g.tensor_tensor(scale[:, :], mv[:, :, 1], conv_cols(layer, which), ALU.mult))
            t = dve("bn_tm", [t], lambda g: g.tensor_tensor(mv[:, :, 0], mv[:, :, 0], scale[:, :], ALU.mult))
            t = dve("bn_tm", [t], lambda g: g.tensor_tensor(shift[:, :], conv_cols(layer, which + 1), mv[:, :, 0], ALU.subtract))
            if b2 is not None:
                t = dve("bn_tm", [t], lambda g: g.tensor_tensor(mv[:, :, 0], b2, scale[:, :], ALU.mult))
                t = dve("bn_tm", [t], lambda g: g.tensor_tensor(shift[:, :], shift[:, :], mv[:, :, 0], ALU.add))
            return t

        tag_mv, w_in, pend = {}, {}, {}

        def chunk_cols(c):
            return u_dram[c, :, :].rearrange("p (k n) -> p k n", k=KC)[:, :, 0:nodes(c)]

        def load_rows(c, u_waits=[]):
            for d, sbuf in rows_of(a["x"], c, xr, False):
                pend["x", c] = dma("sync", "f_ldx", [pend.get(("x1", c - 1))], d, sbuf)
            pend["u", c] = dma("sync", "f_ldu", [pend.get(("turned", c - 1))] + u_waits, u[:, :, 0:nodes(c)], chunk_cols(c))

        def conv_tail(layer, s, store_u=False):
            t = f"c{layer}"
            stats = [z_stats, sb(s, f"{t}_st", [P, KC, NCH, 6])]
            for i in range(2):
                tag_mv[f"{t}{i}"] = sb(s, f"{t}_mv{i}", [P, KC, 2])
            sc1, sh1 = sb(s, f"{t}_sc1", [P, KC]), sb(s, f"{t}_sh1", [P, KC])
            terms = norm_terms(f"{t}0", layer, 1, stats[0], sc1, sh1, [], conv_cols(layer, 0))
            for c0 in range(0, NCH, 2):
                chunks = range(c0, min(c0 + 2, NCH))
                lo, hi_end = c0 * CH, min((c0 + 2) * CH, N)
                for m in range(KC):
                    relu = act("c_u", [terms], lambda g, m=m, lo=lo, hi_end=hi_end: g.activation(
                        agg[:, m, lo:hi_end], agg[:, m, lo:hi_end], ACT.Relu, bias=sh1[:, m:m + 1],
                        scale=sc1[:, m:m + 1]))
                    for c in chunks:
                        st = dve("c_us", [relu], lambda g, m=m, c=c: g.bn_stats(
                            stats[1][:, m, c, :], agg[:, m, c * CH:c * CH + nodes(c)]))
                for c in chunks if store_u else []:
                    u_stored = dma("sync", f"u_st{c > 0:d}", [relu], chunk_cols(c), agg[:, :, c * CH:c * CH + nodes(c)])
                    if c == 0:
                        load_rows(0, [u_stored])
                        for i in range(WB):
                            w_in[i] = load_ffn_weight(i, [])
            if store_u:
                step("sync", stream("fence"), [u_stored], lambda g: g.nop())
            return norm_terms(f"{t}1", layer, 3, stats[1], sc2, sh2, [st])

        aggregate(0)
        with ExitStack() as s:
            w1s, w1_split = split_conv_weight(s, "b_w1", w1[1])
            pH = [ps(s, f"b_ph{i}", [P, TPC, C]) for i in range(2)]
            terms = conv_tail(0, s)
            V = [sb(s, f"b_v{i}", [P, KC, CH]) for i in range(2)]
            VH = [sb(s, f"b_vh{i}", [P, KC, CH], f32r) for i in range(3)]
            VL = [sb(s, f"b_vl{i}", [P, KC, CH], f32r) for i in range(3)]
            H = [xr] + [sb(s, f"b_h{i}", [P, TPC, C]) for i in range(2)]
            v, vt, prod, biased, hst = {}, {}, {}, {}, {}
            for i in range(NCH + 4):
                q = i
                if q < NCH:
                    nn, lo, b = nodes(q), q * CH, q % 2
                    for m in range(KC):
                        v[q] = act("b_v", [terms, vt.get(q - 2)], lambda g, m=m, nn=nn, lo=lo, b=b: g.activation(
                            V[b][:, m, 0:nn], agg[:, m, lo:lo + nn], ACT.Relu, bias=sh2[:, m:m + 1],
                            scale=sc2[:, m:m + 1]))
                    pool("b_clr", [v[q]], lambda g, lo=lo, nn=nn, q=q: g.memset(
                        agg[:, :, lo:(lo + nn if q < NCH - 1 else AW)], 0.0))
                q = i - 1
                if 0 <= q < NCH:
                    nn, b, b3 = nodes(q), q % 2, q % 3
                    h = dve("b_vh", [v[q], prod.get(q - 3)], lambda g, nn=nn, b=b, b3=b3: g.tensor_copy(
                        VH[b3][:, :, 0:nn], V[b][:, :, 0:nn]))
                    vt[q] = dve("b_vl", [h], lambda g, nn=nn, b=b, b3=b3: g.tensor_tensor(
                        VL[b3][:, :, 0:nn], V[b][:, :, 0:nn], VH[b3][:, :, 0:nn].bitcast(fp32), ALU.subtract))
                q = i - 2
                if 0 <= q < NCH:
                    prod[q] = hidden_product("b", q, passes((VH[q % 3], VL[q % 3]), w1s), pH[q % 2],
                                             [vt[q], w1_split, biased.get(q - 2)])
                q = i - 3
                if 0 <= q < NCH:
                    biased[q], hst[q] = hidden_out("b", q, b1_all[1], H[q % 3], pH[q % 2], h_dram[1],
                                                   [prod[q], hst.get(q - 3)])
            last_stores(hst)
            run_block()

        aggregate(1)
        edges.close()
        with ExitStack() as s:
            conv_tail(1, s, store_u=True)
            dve("seen", list(w_in.values()) + [pend["x", 0], pend["u", 0]], lambda g: g.memset(ones_row[0:1, 0:1], 1.0))
            run_block()
        convs.close()

        with ExitStack() as s:
            whi = {n: sb(s, f"{n}_hi", [P, NX, KC, C], f32r) for n in names}
            wlo = {n: sb(s, f"{n}_lo", [P, NX, KC, C], f32r) for n in names}
            wrh, wrl = sb(s, "wrh", [P, KC, P], f32r), sb(s, "wrl", [P, KC, P], f32r)
            scale = [sb(s, f"f_sc{i}", [P, NX * KC]) for i in range(2)]
            shift = [sb(s, f"f_sh{i}", [P, NX * KC]) for i in range(2)]
            x1 = [sb(s, f"f_x{i}", [P, TPC, C]) for i in range(2)]
            y = sb(s, "f_y", [P, TPC, C])
            yhi = [sb(s, f"f_yh{i}", [P, KC, CH], f32r) for i in range(2)]
            ylo = [sb(s, f"f_yl{i}", [P, KC, CH], f32r) for i in range(2)]
            hf = [sb(s, f"f_hf{i}", [P, KC, CH]) for i in range(2)]
            hhi = [[sb(s, f"f_hh{l}{i}", [P, KC, CH], f32r) for i in range(2)] for l in range(2)]
            hlo = [[sb(s, f"f_hl{l}{i}", [P, KC, CH], f32r) for i in range(2)] for l in range(2)]
            ST = sb(s, "f_st", [P, TPC, 6])
            MV = sb(s, "f_mv", [P, TPC, 2])
            lg = sb(s, "f_lg", [P, TPC, NX])
            ex = sb(s, "f_ex", [P, TPC, NX])
            mx = sb(s, "f_mx", [P, TPC])
            sm = sb(s, "f_sm", [P, TPC])
            gate = [sb(s, f"f_gate{i}", [P, TPC, NX]) for i in range(2)]
            lgT = sb(s, "f_lgt", [NX, CH])
            Q = 32
            gT = sb(s, "f_gt", [3 * Q, CH], f32r)
            bo3 = sb(s, "f_bo3", [3 * Q, C], f32r)
            p1 = ps(s, "f_p1", [P, KC, CH])
            p2 = ps(s, "f_p2", [P, KC, CH])
            p3 = ps(s, "f_p3", [P, TPC, C])
            pm = ps(s, "f_pm", [P, KC * CH])

            for l in range(2):
                w = NX * KC
                g_, b_, be_, m_, v_ = (ffn_p[l][:, i * w:(i + 1) * w] for i in range(5))
                t = act("f_sd", [], lambda g, v_=v_: g.activation(v_, v_, ACT.Sqrt, bias=eps_ffn[:, :]))
                t = dve("f_tm", [t], lambda g, v_=v_: g.reciprocal(v_, v_))
                t = dve("f_tm", [t], lambda g, v_=v_, g_=g_, l=l: g.tensor_tensor(scale[l][:, :], v_, g_, ALU.mult))
                t1 = dve("f_tm", [], lambda g, b_=b_, m_=m_: g.tensor_tensor(b_, b_, m_, ALU.subtract))
                t = dve("f_tm", [t1], lambda g, b_=b_, l=l: g.tensor_tensor(b_, b_, scale[l][:, :], ALU.mult))
                terms = dve("f_tm", [t], lambda g, b_=b_, be_=be_, l=l: g.tensor_tensor(shift[l][:, :], b_, be_, ALU.add))
            t = act("f_wr", [], lambda g: g.activation(wrh[:, :, :], wr_raw[:, :, :], ACT.Copy))
            wr_ready = dve("f_wl", [t], lambda g: g.tensor_tensor(
                wrl[:, :, :], wr_raw[:, :, :], wrh[:, :, :].bitcast(fp32), ALU.subtract))

            gT_clear = pool("f_clr", [], lambda g: g.memset(gT[:, :].bitcast(fp32), 0.0))
            bo_clear = pool("f_clr", [], lambda g: g.memset(bo3[:, :].bitcast(fp32), 0.0))
            for q in (0, 2):
                t = act("f_wr", [bo_clear], lambda g, q=q: g.activation(bo3[q * Q:q * Q + NX, :], bo_sb[:, :], ACT.Copy))
            bo_ready = dve("f_wl", [t], lambda g: g.tensor_tensor(
                bo3[Q:Q + NX, :], bo_sb[:, :], bo3[0:NX, :].bitcast(fp32), ALU.subtract))

            w_ready = {}

            def split_weight(i):
                b = i % WB
                n, e = w_order[i]
                hi = act("f_wh", [w_in[i]], lambda g: g.activation(whi[n][:, e, :, :], wst[b][:, :, :], ACT.Copy))
                w_ready[n, e] = dve("f_wl", [hi], lambda g: g.tensor_tensor(
                    wlo[n][:, e, :, :], wst[b][:, :, :], whi[n][:, e, :, :].bitcast(fp32), ALU.subtract))
                if i + WB < len(w_order):
                    w_in[i + WB] = load_ffn_weight(i + WB, [w_ready[n, e]])

            NS = NCH * NX
            y_ready, gate_ready, acc_ready = {}, {}, {}
            l1, l2, l3, h1_ready, h2_ready, p1_free, p2_free, acc, stored = ({} for _ in range(9))
            def pre_residual(c):
                b, nn = c % 2, nodes(c)
                for m in range(KC):
                    q = act("f_q", [pend["u", c]], lambda g, m=m: g.activation(
                        u[:, m, 0:nn], u[:, m, 0:nn], ACT.Identity, bias=sh2[:, m:m + 1], scale=sc2[:, m:m + 1]))
                pend["q", c] = q

            def pre_rows(c):
                b = c % 2
                v = pm[:, :].rearrange("p (j n) -> p j n", n=C)
                pend["turned", c] = t = pe("f_t", [pend["q", c], pend.get(("pm", c - 1))],
                                           [tr(v[0:r, j, k * P:(k + 1) * P], u[:, k, j * P:j * P + r], ident[:, :])
                                            for j, r in tiles(c) for k in range(KC)])
                centered = center("f", c, x1[b], xr, ln1[:, c * TPC:(c + 1) * TPC, :],
                                  [pend["x", c], stored.get(c - 2)], TPC)
                for j, r in tiles(c):
                    a1 = dve("f_a", centered + [t], lambda g, j=j, r=r: g.scalar_tensor_tensor(
                        x1[b][0:r, j, :], x1[b][0:r, j, :], ln1[0:r, c * TPC + j, 1:2], v[0:r, j, :], ALU.mult, ALU.add))
                pend["rows", c] = a1
                for j, k, r in groups(c):
                    pend["x1", c] = dve("f_s", [a1], lambda g, j=j, k=k, r=r: g.scalar_tensor_tensor(
                        x1[b][0:r, j:j + k, :], x1[b][0:r, j:j + k, :], 0.0, xr[0:r, j:j + k, :], ALU.max, ALU.add))

            def pre_norm(c):
                sd = row_stats("f", c, x1[c % 2], ST, MV, [pend["x1", c], pend.get(("y", c - 1))])
                rs = row_rstd("f", c, MV, [sd])
                pend["y", c] = normalize("f", c, y, x1[c % 2], MV, [rs, pend.get(("yt", c - 1))])

            def pre_turn(c):
                b, nn = c % 2, nodes(c)
                pend["yt", c] = t = pe("f_yt", [pend["y", c], pend["rows", c]],
                                       [tr(pm[:, k * CH + j * P:k * CH + j * P + r], y[0:r, j, k * P:(k + 1) * P],
                                           ident[0:r, 0:r]) for j, r in tiles(c) for k in range(KC)])
                v = pm[:, :].rearrange("p (k n) -> p k n", k=KC)[:, :, 0:nn]
                h = act("f_yh", [t, l1.get(c * NX - NX - 1)], lambda g: g.activation(yhi[b][:, :, 0:nn], v, ACT.Copy))
                y_ready[c] = dve("f_yl", [h], lambda g: g.tensor_tensor(
                    ylo[b][:, :, 0:nn], v, yhi[b][:, :, 0:nn].bitcast(fp32), ALU.subtract))

            def pre_logits(c):
                b, nn = c % 2, nodes(c)
                pr = passes((yhi[b], ylo[b]), (wrh, wrl))
                t = pe("f_lg", [y_ready[c], wr_ready],
                       [mm(pm[:, 0:nn], w[:, k, :], u[:, k, 0:nn], i == 0 and k == 0, i == 2 and k == KC - 1)
                        for i, (u, w) in enumerate(pr) for k in range(KC)])
                pend["lgt", c] = act("f_lt", [t, pend.get(("lg", c - 1))], lambda g: g.activation(
                    lgT[:, 0:nn], pm[0:NX, 0:nn], ACT.Identity, bias=br_col[:, :]))

            def pre_gate(c):
                b = c % 2
                lgp = pm[:, CH:CH + TPC * NX].rearrange("p (j e) -> p j e", e=NX)
                t = pe("f_lr", [pend["lgt", c]],
                       [tr(lgp[0:r, j, :], lgT[:, j * P:j * P + r], ident[0:NX, 0:NX]) for j, r in tiles(c)])
                for j, k, r in groups(c):
                    t1 = dve("f_g", [t, pend.get(("ex", c - 1))], lambda g, j=j, k=k, r=r: g.tensor_copy(
                        lg[0:r, j:j + k, :], lgp[0:r, j:j + k, :]))
                pend["lg", c] = t1
                for j, k, r in groups(c):
                    t2 = dve("f_g", [t1], lambda g, j=j, k=k, r=r: g.tensor_reduce(
                        mx[0:r, j:j + k], lg[0:r, j:j + k, :], AX.X, ALU.max))
                for j, k, r in groups(c):
                    t3 = dve("f_g", [t2], lambda g, j=j, k=k, r=r: g.tensor_tensor(
                        lg[0:r, j:j + k, :], lg[0:r, j:j + k, :],
                        mx[0:r, j:j + k].unsqueeze(2).broadcast_to([r, k, NX]), ALU.subtract))
                for j, k, r in groups(c):
                    t4 = act("f_ex", [t3, gate_ready.get(c - 1)], lambda g, j=j, k=k, r=r: g.activation(
                        ex[0:r, j:j + k, :], lg[0:r, j:j + k, :], ACT.Exp))
                pend["ex", c] = t4
                for j, k, r in groups(c):
                    t5 = dve("f_g", [t4], lambda g, j=j, k=k, r=r: g.tensor_reduce(
                        sm[0:r, j:j + k], ex[0:r, j:j + k, :], AX.X, ALU.add))
                for j, k, r in groups(c):
                    t6 = dve("f_g", [t5], lambda g, j=j, k=k, r=r: g.reciprocal(sm[0:r, j:j + k], sm[0:r, j:j + k]))
                for j, k, r in groups(c):
                    gate_ready[c] = dve("f_g", [t6], lambda g, j=j, k=k, r=r, b=b: g.tensor_tensor(
                        gate[b][0:r, j:j + k, :], ex[0:r, j:j + k, :],
                        sm[0:r, j:j + k].unsqueeze(2).broadcast_to([r, k, NX]), ALU.mult))

            def pre_bias_turn(c):
                b, nn = c % 2, nodes(c)
                t = pe("f_gt", [gate_ready[c]],
                       [tr(pm[0:NX, CH + j * P:CH + j * P + r], gate[b][0:r, j, :], ident[0:r, 0:r]) for j, r in tiles(c)])
                src = pm[0:NX, CH:CH + nn]
                for q in range(2):
                    h = act("f_ge", [t, gT_clear, pend.get(("bo", c - 1))], lambda g, q=q: g.activation(
                        gT[q * Q:q * Q + NX, 0:nn], src, ACT.Copy))
                pend["gt", c] = dve("f_gl", [h], lambda g: g.tensor_tensor(
                    gT[2 * Q:2 * Q + NX, 0:nn], src, gT[0:NX, 0:nn].bitcast(fp32), ALU.subtract))

            def pre_bias(c):
                b = c % 2
                v = pm[:, :].rearrange("p (j n) -> p j n", n=C)
                pend["bo", c] = t = pe("f_bo", [pend["gt", c], pend["lg", c], bo_ready],
                                       [mm(v[0:r, j, :], gT[:, j * P:j * P + r], bo3[:, :], True, True) for j, r in tiles(c)])
                for j, k, r in groups(c):
                    pend["pm", c] = acc_ready[c] = dve("f_ac", [t], lambda g, j=j, k=k, r=r: g.tensor_tensor(
                        x1[b][0:r, j:j + k, :], v[0:r, j:j + k, :], x1[b][0:r, j:j + k, :], ALU.add))

            def three(w, xh, xl, e, c, o):
                nn = nodes(c)
                pr = [(whi[w], xh), (whi[w], xl), (wlo[w], xh)]
                return [mm(o[:, m, 0:nn], ww[:, e, k, m * P:(m + 1) * P], xx[:, k, 0:nn], i == 0 and k == 0,
                           i == 2 and k == KC - 1)
                        for m in range(KC) for i, (ww, xx) in enumerate(pr) for k in range(KC)]

            def hidden(l, p, prod, i, c, e, reader):
                nn, b = nodes(c), i % 2
                for m in range(KC):
                    col = slice(e * KC + m, e * KC + m + 1)
                    hi = act(f"f_a{l}", [prod, reader, terms], lambda g, m=m, col=col: g.activation(
                        hhi[l][b][:, m, 0:nn], p[:, m, 0:nn], ACT.Relu, bias=shift[l][:, col], scale=scale[l][:, col]))
                for m in range(KC):
                    col = slice(e * KC + m, e * KC + m + 1)
                    full = act(f"f_a{l}", [pend.get(("lo", l))], lambda g, m=m, col=col: g.activation(
                        hf[l][:, m, 0:nn], p[:, m, 0:nn], ACT.Relu, bias=shift[l][:, col], scale=scale[l][:, col]))
                lo = dve(f"f_l{l}", [full], lambda g: g.tensor_tensor(
                    hlo[l][b][:, :, 0:nn], hf[l][:, :, 0:nn], hhi[l][b][:, :, 0:nn].bitcast(fp32), ALU.subtract))
                pend["lo", l] = lo
                return full, lo

            split_weight(0)
            pre_residual(0)
            pre_rows(0)
            pre_norm(0)
            pre_turn(0)
            for n in range(1, len(names)):
                split_weight(n)
            for i in range(NS + 2):
                c, e = divmod(i, NX)
                if i < NS:
                    l1[i] = pe("f_m1", [y_ready[c], w_ready["W1", e], p1_free.get(i - 1)],
                               three("W1", yhi[c % 2], ylo[c % 2], e, c, p1))
                    p1_free[i], h1_ready[i] = hidden(0, p1, l1[i], i, c, e, l2.get(i - 2))
                    if i == 0:
                        pre_logits(0)
                        load_rows(1)
                    if i == 1:
                        pre_gate(0)
                    if i == 2:
                        pre_bias(0)
                    if c + 1 < NCH:
                        if e == 3:
                            pre_rows(c + 1)
                        if e == 4:
                            pre_norm(c + 1)
                        if e == 5:
                            pre_turn(c + 1)
                        if e == 6:
                            pre_logits(c + 1)
                        if e == 7:
                            pre_gate(c + 1)
                    if e == 0 and c > 0:
                        pre_bias_turn(c)
                    if e == 1 and c > 0:
                        pre_bias(c)
                    if e == 1 and 0 < c < NCH - 1:
                        load_rows(c + 1)
                    if e == 2 and c + 1 < NCH:
                        pre_residual(c + 1)
                    if i == 0:
                        for n in range(len(names)):
                            split_weight(len(names) + n)
                if 1 <= i <= NS:
                    q = i - 1
                    cq, eq = divmod(q, NX)
                    l2[q] = pe("f_m2", [h1_ready[q], w_ready["W2", eq], p2_free.get(q - 1)],
                               three("W2", hhi[0][q % 2], hlo[0][q % 2], eq, cq, p2))
                    p2_free[q], h2_ready[q] = hidden(1, p2, l2[q], q, cq, eq, l3.get(q - 2))
                if i == 1:
                    pre_bias_turn(0)
                if i < NX - 2:
                    for n in range(len(names)):
                        split_weight(len(names) * (i + 2) + n)
                if i >= 2:
                    q = i - 2
                    cq, eq = divmod(q, NX)
                    b = q % 2
                    pr = [(hhi[1][b], whi["Wo"]), (hhi[1][b], wlo["Wo"]), (hlo[1][b], whi["Wo"])]
                    l3[q] = pe("f_m3", [h2_ready[q], w_ready["Wo", eq], acc.get(q - 1)],
                               [mm(p3[0:r, j, :], xx[:, k, j * P:j * P + r], ww[:, eq, k, :], n == 0 and k == 0,
                                   n == 2 and k == KC - 1)
                                for j, r in tiles(cq) for n, (xx, ww) in enumerate(pr) for k in range(KC)])
                    for j, r in tiles(cq):
                        acc[q] = dve("f_c3", [l3[q], acc_ready[cq] if eq == 0 else acc[q - 1]],
                                     lambda g, j=j, r=r, cq=cq, eq=eq: g.scalar_tensor_tensor(
                                         x1[cq % 2][0:r, j, :], p3[0:r, j, :], gate[cq % 2][0:r, j, eq:eq + 1],
                                         x1[cq % 2][0:r, j, :], ALU.mult, ALU.add))
                    if eq == NX - 1:
                        for d, sbuf in rows_of(out, cq, x1[cq % 2], True):
                            stored[cq] = dma("sync", f"f_st{cq % 2}", [acc[q]], d, sbuf)
            step("sync", stream("fence"), [stored[NCH - 1], stored[NCH - 2]], lambda g: g.nop())
            run_block()


def kernel(**inputs):
    import numpy as np
    import concourse.bacc as bacc
    from concourse import mybir
    from concourse.bass_utils import run_bass_kernel_spmd

    nc = bacc.Bacc("TRN2", target_bir_lowering=False, num_devices=1)
    arrays, aps = {}, {}
    for name, value in inputs.items():
        v = np.ascontiguousarray(value)
        arrays[f"in_{name}"] = v
        aps[name] = nc.dram_tensor(f"in_{name}", v.shape, mybir.dt.from_np(v.dtype), kind="ExternalInput").ap()
    out = nc.dram_tensor("out_x", arrays["in_x"].shape, mybir.dt.float32, kind="ExternalOutput").ap()
    build(nc, aps, out)
    r = run_bass_kernel_spmd(nc, [arrays], core_ids=[0])
    return r.results[0]["out_x"]
```
